# Optimizing a Trainium2 kernel written in Bass

```python
import numpy as np
import jax
import jax.numpy as jnp

def _softmax(x, axis=-1):
    return jax.nn.softmax(x, axis=axis)

def _gelu(x):
    return jax.nn.gelu(x, approximate=True)

def _silu(x):
    return jax.nn.silu(x)

def _sigmoid(x):
    return jax.nn.sigmoid(x)

def _layernorm(x, axis=-1, eps=1e-05):
    m = jnp.mean(x, axis=axis, keepdims=True)
    v = jnp.var(x, axis=axis, keepdims=True)
    return (x - m) / jnp.sqrt(v + eps)

def _scatter_add(tgt, idx, src, axis=0):
    return tgt.at[idx].add(src)

def _segment_sum(src, seg, n):
    return jax.ops.segment_sum(src, seg, n)
kernel_name = 'mk_gnn_preln_d2_gnn_r32_41289d'

def setup_inputs(seed: int=0):
    np.random.seed(seed)
    _w = jnp.asarray

    def _rec_inputs():
        import jax
        import jax.numpy as jnp
        _gk = jax.random.key(seed)
        x = -0.0002117 + 1 * jax.random.normal(jax.random.fold_in(_gk, 1), (3125, 256), jnp.float32)
        src = jax.random.randint(jax.random.fold_in(_gk, 2), (50000,), 0, 3125, jnp.int32)
        dst = jax.random.randint(jax.random.fold_in(_gk, 3), (50000,), 0, 3125, jnp.int32)
        _o = jnp.argsort(dst, stable=True)
        src = src[_o]
        dst = dst[_o]
        edge_type_2 = jax.random.randint(jax.random.fold_in(_gk, 12), (50000,), 0, 2, jnp.int32)
        edge_weight = jax.random.uniform(jax.random.fold_in(_gk, 13), (50000,), jnp.float32, 0.0, 1)
        return (x, src, dst, edge_type_2, edge_weight)
    x, src, dst, edge_type_2, edge_weight = _rec_inputs()

    def _L0_gnn_setup():
        import jax, jax.numpy as jnp
        import numpy as np
        N_NODES = 3125
        N_EDGES = 100000
        D = 256

        def _graph_conv(x, W, edge_src, edge_dst, edge_weight, n_nodes):
            support = x @ W
            msg = support[edge_src] * edge_weight[:, None]
            return jax.ops.segment_sum(msg, edge_dst, num_segments=n_nodes)
        key = jax.random.key(seed)
        k1, k2, k3, k4, k5, k6 = jax.random.split(key, 6)
        scale = 1.0 / np.sqrt(D)
        return {'features': jax.random.normal(k1, (N_NODES, D), dtype=jnp.float32), 'edge_weight': jax.random.uniform(k2, (N_EDGES,), dtype=jnp.float32), 'W1': jax.random.normal(k3, (D, D), dtype=jnp.float32) * scale, 'W2': jax.random.normal(k4, (D, D), dtype=jnp.float32) * scale, 'edge_src': jax.random.randint(k5, (N_EDGES,), 0, N_NODES, dtype=jnp.int32), 'edge_dst': jax.random.randint(k6, (N_EDGES,), 0, N_NODES, dtype=jnp.int32)}
    _L0_gnn_all = _L0_gnn_setup()
    _L0_gnn_in = {k: v for k, v in _L0_gnn_all.items() if k in ('W1', 'W2')}
    del _L0_gnn_all

    def _L1_gnn_setup():
        import jax, jax.numpy as jnp
        import numpy as np
        N_NODES = 10000
        N_EDGES = 10000
        D = 256
        D_OUT = 256
        NUM_REL = 2
        key = jax.random.key(seed)
        ks = jax.random.split(key, 16)
        s = 1.0 / np.sqrt(D)
        inp = {}
        inp['feat'] = jax.random.normal(ks[0], (N_NODES, D), dtype=jnp.float32)
        inp['src'] = jax.random.randint(ks[1], (N_EDGES,), 0, N_NODES, dtype=jnp.int32)
        inp['dst'] = jax.random.randint(ks[2], (N_EDGES,), 0, N_NODES, dtype=jnp.int32)
        inp['rel'] = jax.random.randint(ks[3], (N_EDGES,), 0, NUM_REL, dtype=jnp.int32)
        inp['W_rel'] = jax.random.normal(ks[4], (NUM_REL, D, D), dtype=jnp.float32) * s
        inp['b_rel'] = jax.random.normal(ks[5], (NUM_REL, D), dtype=jnp.float32) * s
        inp['W_ih'] = jax.random.normal(ks[6], (4 * D, D), dtype=jnp.float32) * s
        inp['b_ih'] = jax.random.normal(ks[7], (4 * D,), dtype=jnp.float32) * s
        inp['b_hh'] = jax.random.normal(ks[8], (4 * D,), dtype=jnp.float32) * s
        h = D // 2
        inp['W1'] = jax.random.normal(ks[9], (h, D), dtype=jnp.float32) * s
        inp['b1'] = jax.random.normal(ks[10], (h,), dtype=jnp.float32) * s
        inp['W2'] = jax.random.normal(ks[11], (h, h), dtype=jnp.float32) * (1.0 / np.sqrt(h))
        inp['b2'] = jax.random.normal(ks[12], (h,), dtype=jnp.float32) * (1.0 / np.sqrt(h))
        inp['W3'] = jax.random.normal(ks[13], (D_OUT, h), dtype=jnp.float32) * (1.0 / np.sqrt(h))
        inp['b3'] = jax.random.normal(ks[14], (D_OUT,), dtype=jnp.float32) * (1.0 / np.sqrt(h))
        return inp
    _L1_gnn_all = _L1_gnn_setup()
    _L1_gnn_in = {k: v for k, v in _L1_gnn_all.items() if k in ('W_rel', 'b_rel', 'W_ih', 'b_ih', 'b_hh', 'W1', 'b1', 'W2', 'b2', 'W3', 'b3')}
    del _L1_gnn_all
    return {'x': x, 'src': src, 'dst': dst, 'edge_type_2': edge_type_2, 'edge_weight': edge_weight, 'L0_gnn_W1': _L0_gnn_in['W1'], 'L0_gnn_W2': _L0_gnn_in['W2'], 'L1_gnn_W_rel': _L1_gnn_in['W_rel'], 'L1_gnn_b_rel': _L1_gnn_in['b_rel'], 'L1_gnn_W_ih': _L1_gnn_in['W_ih'], 'L1_gnn_b_ih': _L1_gnn_in['b_ih'], 'L1_gnn_b_hh': _L1_gnn_in['b_hh'], 'L1_gnn_W1': _L1_gnn_in['W1'], 'L1_gnn_b1': _L1_gnn_in['b1'], 'L1_gnn_W2': _L1_gnn_in['W2'], 'L1_gnn_b2': _L1_gnn_in['b2'], 'L1_gnn_W3': _L1_gnn_in['W3'], 'L1_gnn_b3': _L1_gnn_in['b3']}

def reference(x, src, dst, edge_type_2, edge_weight, L0_gnn_W1, L0_gnn_W2, L1_gnn_W_rel, L1_gnn_b_rel, L1_gnn_W_ih, L1_gnn_b_ih, L1_gnn_b_hh, L1_gnn_W1, L1_gnn_b1, L1_gnn_W2, L1_gnn_b2, L1_gnn_W3, L1_gnn_b3):
    import jax
    import jax.numpy as jnp

    def _L0_gnn_ref(features, edge_weight, W1, W2, edge_src, edge_dst):
        import jax, jax.numpy as jnp
        import numpy as np
        N_NODES = 3125
        N_EDGES = 100000
        D = 256

        def _graph_conv(x, W, edge_src, edge_dst, edge_weight, n_nodes):
            support = x @ W
            msg = support[edge_src] * edge_weight[:, None]
            return jax.ops.segment_sum(msg, edge_dst, num_segments=n_nodes)
        n = features.shape[0]
        h = _graph_conv(features, W1, edge_src, edge_dst, edge_weight, n)
        out = _graph_conv(h, W2, edge_src, edge_dst, edge_weight, n)
        return out

    def _L1_gnn_ref(feat, src, dst, rel, W_rel, b_rel, W_ih, b_ih, b_hh, W1, b1, W2, b2, W3, b3):
        import jax, jax.numpy as jnp
        import numpy as np
        N_NODES = 10000
        N_EDGES = 10000
        D = 256
        D_OUT = 256
        NUM_REL = 2
        n_nodes = feat.shape[0]
        S = feat[src]

        def edge_nn(x, W, b):
            h = jax.nn.relu(x @ W.T + b)
            return jax.nn.relu(h @ W.T + b)
        msgs = jnp.zeros_like(S)
        for r in range(W_rel.shape[0]):
            msgs = jnp.where((rel == r)[:, None], edge_nn(S, W_rel[r], b_rel[r]), msgs)
        agg = jax.ops.segment_sum(msgs, dst, num_segments=n_nodes)
        gates = agg @ W_ih.T + b_ih + b_hh
        i, f, g, o = jnp.split(gates, 4, axis=-1)
        c = jax.nn.sigmoid(i) * jnp.tanh(g)
        hn = jax.nn.sigmoid(o) * jnp.tanh(c)
        x = jax.nn.relu(hn @ W1.T + b1)
        x = jax.nn.relu(x @ W2.T + b2)
        return x @ W3.T + b3
    h = jnp.maximum(_layernorm(x, axis=-1), 0.0)
    x = x + _L0_gnn_ref(h, edge_weight, L0_gnn_W1, L0_gnn_W2, src, dst)
    h = jnp.maximum(_layernorm(x, axis=-1), 0.0)
    x = x + _L1_gnn_ref(h, src, dst, edge_type_2, L1_gnn_W_rel, L1_gnn_b_rel, L1_gnn_W_ih, L1_gnn_b_ih, L1_gnn_b_hh, L1_gnn_W1, L1_gnn_b1, L1_gnn_W2, L1_gnn_b2, L1_gnn_W3, L1_gnn_b3)
    return x

_drawn_inputs = setup_inputs


def setup_inputs(seed=0):
    import zlib

    import numpy as np

    out = dict(_drawn_inputs(seed))
    spreads = {}
    factors = {'L1_gnn_W_rel': 8.0,
     'L1_gnn_b_rel': 8.0,
     'L1_gnn_W_ih': 8.0,
     'L1_gnn_b_ih': 34.61,
     'L1_gnn_b_hh': 28.381,
     'L1_gnn_W1': 8.0,
     'L1_gnn_b1': 8.0,
     'L1_gnn_W2': 8.0,
     'L1_gnn_b2': 8.0,
     'L1_gnn_W3': 8.0,
     'L1_gnn_b3': 53.199}
    for name, (base, spread) in spreads.items():
        noise = np.random.default_rng([zlib.crc32(name.encode()), seed]).standard_normal(out[name].shape)
        drawn = base * np.exp(spread * noise) if base else spread * noise
        out[name] = jnp.asarray(drawn.astype(out[name].dtype))
    for name, factor in factors.items():
        out[name] = (out[name] * factor).astype(out[name].dtype)
    return out
```

```python
from contextlib import ExitStack

import numpy as np

import concourse.bass as bass
from concourse import mybir

F32 = mybir.dt.float32
I32 = mybir.dt.int32
ALU = mybir.AluOpType
ACT = mybir.ActivationFunctionType
AX_X = mybir.AxisListType.X

P = 128
N_NODES = 3125
N_EDGES = 50000
D = 256
K = D // P
CHUNKS = -(-N_NODES // P)
NODES = CHUNKS * P
LAST_ROWS = N_NODES - (CHUNKS - 1) * P
TILES = -(-N_EDGES // P)
BLOCK = 8
BLOCKS = -(-TILES // BLOCK)
COLS = BLOCKS * BLOCK
ROUND = 2 * BLOCK
ROUNDS = TILES // ROUND
TAIL = TILES - ROUNDS * ROUND
SPAN = 32
SIDE = P // SPAN
MARGIN = BLOCK
BANKS = 4
PROPS = 3
REL = 2
HALF = D // 2
EPS = 1e-5
GROUPS = 5
GC = CHUNKS // GROUPS
PAD_REL = REL


def build(nc, x, src_t, dst_t, dst_seq, rel_t, weight_t, w_prop1, w_prop2, w_rel_t, b_rel_cols, b_rel_row,
          w_ih_t, b_ih_cols, b_hh_cols, w_mlp1, b_mlp1, w_mlp2, b_mlp2, w_mlp3, b_mlp3, out):
    with ExitStack() as ctx:
        def sb(name, shape, dt=F32):
            return ctx.enter_context(nc.sbuf_tensor(name, shape, dt))

        def bank(name):
            return ctx.enter_context(nc.psum_tensor(name, [P, 512], F32))

        def sem(name):
            return ctx.enter_context(nc.semaphore(name))

        table = [nc.dram_tensor("table_hidden", (NODES, D), F32, kind="Internal").ap(),
                 nc.dram_tensor("table_mid", (NODES, D), F32, kind="Internal").ap(),
                 nc.dram_tensor("table_messages", (REL * NODES, D), F32, kind="Internal").ap()]

        nodes = sb("nodes", [P, CHUNKS * D])
        acc = sb("acc", [P, K, NODES])
        rows = sb("rows", [P, ROUND, D])
        src_idx = sb("src_idx", [P, COLS], I32)
        msg_idx = sb("msg_idx", [P, COLS], I32)
        dst_i = sb("dst_i", [P, COLS], I32)
        rel_i = sb("rel_i", [P, COLS], I32)
        weight = sb("weight", [P, COLS])
        known = sb("known", [P, COLS])
        dst_f = sb("dst_f", [P, COLS])
        dst_off = sb("dst_off", [P, COLS])
        seq_i = sb("seq_i", [P, TILES + 1], I32)
        seq_f = sb("seq_f", [P, TILES + 1])
        steps = sb("steps", [P, TILES])
        idx_stage = sb("idx_stage", [P, ROUND], I32)
        sel = sb("sel", [P, ROUND, SPAN])
        sel_wide = sb("sel_wide", [P, P])
        iota_i = sb("iota_i", [P, NODES], I32)
        iota_f = sb("iota_f", [P, NODES])
        final_cols = sb("final_cols", [P, ROUNDS - 1])
        final_i = sb("final_i", [P, ROUNDS - 1], I32)
        zeros = sb("zeros", [P, K, P])
        ones = sb("ones", [P, P])
        identity = sb("identity", [P, P])
        eps = sb("eps", [P, 1])
        flags = sb("flags", [P, 4])
        flag_sum = sb("flag_sum", [P, 1])
        far = sb("far", [P, ROUNDS - 1])
        disorder = sb("disorder", [P, 1], I32)

        w_prop = [sb("w_prop1_sb", [P, K, D]), sb("w_prop2_sb", [P, K, D])]
        w_rel = sb("w_rel_sb", [P, REL, K, D])
        b_rel_c = sb("b_rel_c", [P, REL * K])
        b_rel_r = sb("b_rel_r", [1, REL * D])
        w_ih = sb("w_ih_sb", [P, K, 4 * D])
        b_ih = sb("b_ih_sb", [P, 4 * K])
        b_hh = sb("b_hh_sb", [P, 4 * K])
        b_gate = sb("b_gate", [P, 4 * K])
        w1 = sb("w1_sb", [P, K, HALF])
        b1 = sb("b1_sb", [HALF, 1])
        w2 = sb("w2_sb", [HALF, HALF])
        b2 = sb("b2_sb", [HALF, 1])
        w3 = sb("w3_sb", [HALF, D])
        b3 = sb("b3_sb", [1, D])

        sums = sb("sums", [P, K, P])
        out_rows = [sb("out_rows0", [P, REL, D]), sb("out_rows1", [P, REL, D])]
        bn = sb("bn", [P, CHUNKS, 6])
        mean_var = sb("mean_var", [P, CHUNKS, 2])
        std = sb("std", [P, CHUNKS])
        rstd = sb("rstd", [P, CHUNKS])
        shift = sb("shift", [P, CHUNKS])
        hidden = sb("hidden", [P, D])
        hidden_t = sb("hidden_t", [P, K, P])
        rel1_t = sb("rel1_t", [P, REL, K, P])
        gate_i = sb("gate_i", [P, K, P])
        gate_g = sb("gate_g", [P, K, P])
        gate_o = sb("gate_o", [P, K, P])
        cell = sb("cell", [P, K, P])
        cell_tanh = sb("cell_tanh", [P, K, P])
        lstm_t = sb("lstm_t", [P, K, P])
        mlp1_t = sb("mlp1_t", [HALF, P])
        mlp2_t = sb("mlp2_t", [HALF, P])

        tile_ps = [bank(f"tile_ps{i}") for i in range(BANKS)]
        iota_ps = bank("iota_ps")
        ps_a, ps_b, ps_c = bank("ps_a"), bank("ps_b"), bank("ps_c")
        iota_cols = iota_ps[:, 0:BLOCK * SPAN].rearrange("p (t n) -> p t n", n=SPAN)
        one_hot = iota_ps[:, BLOCK * SPAN:2 * BLOCK * SPAN].rearrange("p (t n) -> p t n", n=SPAN)

        edges_in, seq_in, weights_in = sem("edges_in"), sem("seq_in"), sem("weights_in")
        x_in = [sem(f"x_in{g}") for g in range(GROUPS)]
        iota_made, const_made, zero_made, identity_made = (
            sem("iota_made"), sem("const_made"), sem("zero_made"), sem("identity_made"))
        settled = sem("settled")
        iota_ready, bias_ready = sem("iota_ready"), sem("bias_ready")
        edge_step = sem("edge_step")
        starts_ready, flags_ready, disorder_summed, path_ready = (
            sem("starts_ready"), sem("flags_ready"), sem("disorder_summed"), sem("path_ready"))
        group_bn, group_stats, group_std, group_rstd, group_shift, group_hidden = (
            sem("group_bn"), sem("group_stats"), sem("group_std"), sem("group_rstd"), sem("group_shift"),
            sem("group_hidden"))
        hidden_stored = [sem(f"hidden_stored{g}") for g in range(GROUPS)]
        table_stored = [sem(f"table_stored{p}") for p in range(PROPS)]
        staged = [sem(f"staged{h}") for h in range(2)]
        gathered = [sem(f"gathered{s}") for s in range(ROUND)]
        hot_ready, sel_ready, product_done, added = (
            sem("hot_ready"), sem("sel_ready"), sem("product_done"), sem("added"))
        wide_staged, wide_gathered, wide_sel, wide_product, wide_added = (
            sem("wide_staged"), sem("wide_gathered"), sem("wide_sel"), sem("wide_product"), sem("wide_added"))
        sums_ready, acc_cleared, dense_done = sem("sums_ready"), sem("acc_cleared"), sem("dense_done")
        rows_ready = sem("rows_ready")
        x2_ready, bn_ready, stats_ready, std_ready, rstd_ready, shift_ready, hidden_ready = (
            sem("x2_ready"), sem("bn_ready"), sem("stats_ready"), sem("std_ready"), sem("rstd_ready"),
            sem("shift_ready"), sem("hidden_ready"))
        turned, turned_copied, rel1_done, rel1_ready, rel2_done = (
            sem("turned"), sem("turned_copied"), sem("rel1_done"), sem("rel1_ready"), sem("rel2_done"))
        gates_ready, cell_ready, cell_tanh_ready, lstm_ready = (
            sem("gates_ready"), sem("cell_ready"), sem("cell_tanh_ready"), sem("lstm_ready"))
        mlp1_done, mlp1_ready, mlp2_done, mlp2_ready, mlp3_done, y_ready, y_stored = (
            sem("mlp1_done"), sem("mlp1_ready"), sem("mlp2_done"), sem("mlp2_ready"), sem("mlp3_done"),
            sem("y_ready"), sem("y_stored"))

        WEIGHTS = 14

        def path(eng):
            eng.wait_ge(path_ready, 1)
            return nc.values_load(disorder[0:1, 0:1], engines=[eng.engine], min_val=0, max_val=1 << 20,
                                  skip_runtime_bounds_check_because="a count of flags, never negative")

        def settle(eng):
            eng.sem_inc(settled, 1)

        def chunk_cols(c):
            return acc[:, :, bass.ds(c * P, P)]

        def chunk_nodes(c):
            return nodes[:, bass.ds(c * D, D)]

        def pair(ps):
            return ps[:, 0:K * P].rearrange("p (k n) -> p k n", k=K)

        block = ctx.enter_context(nc.Block())

        @block.sync
        def _(sp):
            for to, of in ((dst_i, dst_t), (src_idx, src_t), (rel_i, rel_t), (weight, weight_t)):
                sp.dma_start(to[:, :], of).then_inc(edges_in, 16)
            sp.dma_start(seq_i[:, :], dst_seq).then_inc(seq_in, 16)
            for g in range(GROUPS):
                sp.dma_start(nodes[:, g * GC * D:(g + 1) * GC * D].rearrange("p (c f) -> p c f", f=D),
                             x.rearrange("(c p) f -> p c f", p=P)[:, g * GC:(g + 1) * GC, :]).then_inc(x_in[g], 16)
            for to, of in ((w_prop[0], w_prop1), (w_prop[1], w_prop2), (w_rel, w_rel_t), (b_rel_c, b_rel_cols),
                           (b_rel_r, b_rel_row), (w_ih, w_ih_t), (b_ih, b_ih_cols), (b_hh, b_hh_cols),
                           (w1, w_mlp1), (b1, b_mlp1), (w2, w_mlp2), (b2, b_mlp2), (w3, w_mlp3), (b3, b_mlp3)):
                sp.dma_start(to[:], of).then_inc(weights_in, 16)

            def stage(p, b, half):
                index = msg_idx if p == 2 else src_idx
                sp.dma_start(idx_stage[:, half * BLOCK:(half + 1) * BLOCK],
                             index[:, bass.ds(b * BLOCK, BLOCK)]).then_inc(staged[half], 16)

            sp.wait_ge(edges_in, 64)
            disordered = path(sp)
            with sp.If(disordered == 0):
                for p in range(PROPS):
                    if p > 0:
                        sp.wait_ge(product_done, TILES * p)
                    stage(p, 0, 0)
                    stage(p, 1, 1)
                    with sp.Fori(1, ROUNDS) as i:
                        sp.wait_ge(product_done, TILES * p + i * ROUND - BLOCK)
                        stage(p, 2 * i, 0)
                        sp.wait_ge(product_done, TILES * p + i * ROUND)
                        stage(p, 2 * i + 1, 1)
                    sp.wait_ge(product_done, TILES * p + ROUNDS * ROUND - BLOCK)
                    stage(p, BLOCKS - 1, 0)
            with sp.Else():
                for p in range(PROPS):
                    index = msg_idx if p == 2 else src_idx
                    with sp.Fori(0, TILES) as j:
                        sp.dma_start(idx_stage[:, 0:1], index[:, bass.ds(j, 1)]).then_inc(wide_staged, 16)
                        sp.wait_ge(wide_gathered, (j + (TILES * p + 1)) * 16)
                        settle(sp)
            sp.wait_ge(y_stored, 16 * CHUNKS)

        @block.gpsimd
        def _(pool):
            nc.gpsimd.iota(iota_i[:, :], pattern=[[1, NODES]], base=0, channel_multiplier=0).then_inc(iota_made, 1)
            nc.gpsimd.iota(final_i[:, :], pattern=[[P, ROUNDS - 1]], base=P, channel_multiplier=0)\
                .then_inc(iota_made, 1)
            nc.gpsimd.memset(ones[:, :], 1.0).then_inc(const_made, 1)
            nc.gpsimd.memset(eps[:, :], EPS).then_inc(const_made, 1)
            nc.gpsimd.memset(zeros[:], 0.0).then_inc(const_made, 1)
            nc.gpsimd.memset(identity[:, :], 0.0).then_inc(zero_made, 1)
            nc.gpsimd.memset(acc[:], 0.0).then_inc(const_made, 1)
            pool.wait_ge(zero_made, 1)
            nc.gpsimd.affine_select(out=identity[:, :], in_=identity[:, :], compare_op=ALU.not_equal, fill=1.0,
                                    base=0, pattern=[[-1, P]], channel_multiplier=1).then_inc(identity_made, 1)

            def table_complete(p):
                if p == 0:
                    for g in range(GROUPS):
                        pool.wait_ge(hidden_stored[g], 16)
                else:
                    pool.wait_ge(table_stored[p], 16 * CHUNKS)

            def gather(p, s, out_sem):
                pool.indirect_dma_start(rows[:, s, :], None, table[p][:, :],
                                        bass.IndirectOffsetOnAxis(ap=idx_stage[:, s:s + 1], axis=0))\
                    .then_inc(out_sem, 16)

            def round_(p, i, first, tiles):
                for s in range(tiles):
                    if s % BLOCK == 0:
                        half = s // BLOCK
                        uses = ROUNDS + (1 if half * BLOCK < TAIL else 0)
                        pool.wait_ge(staged[half], (i + (uses * p + 1)) * 16)
                    if s % 4 == 0 and not first:
                        pool.wait_ge(product_done, i * ROUND + (TILES * p - ROUND + min(s + 4, tiles)))
                        settle(pool)
                    gather(p, s, gathered[s])

            disordered = path(pool)
            with pool.If(disordered == 0):
                for p in range(PROPS):
                    table_complete(p)
                    round_(p, 0, True, ROUND)
                    with pool.Fori(1, ROUNDS) as i:
                        round_(p, i, False, ROUND)
                    round_(p, ROUNDS, False, TAIL)
            with pool.Else():
                for p in range(PROPS):
                    table_complete(p)
                    with pool.Fori(0, TILES) as j:
                        pool.wait_ge(wide_staged, (j + (TILES * p + 1)) * 16)
                        settle(pool)
                        gather(p, 0, wide_gathered)
                        pool.wait_ge(wide_product, (j + (TILES * p + 1)) * CHUNKS)

        @block.vector
        def _(dve):
            dve.wait_ge(edges_in, 64)
            nc.vector.tensor_copy(dst_f[:, :], dst_i[:, :]).then_inc(edge_step, 1)
            dve.wait_ge(iota_made, 2)
            nc.vector.tensor_copy(final_cols[:, :], final_i[:, :]).then_inc(edge_step, 1)
            nc.vector.tensor_copy(iota_f[:, :], iota_i[:, :]).then_inc(iota_ready, 1)
            for t in range(BLOCK):
                nc.vector.tensor_copy(iota_cols[:, t, :], iota_i[:, 0:SPAN]).then_inc(iota_ready, 1)
            nc.vector.tensor_scalar(msg_idx[:, :], rel_i[:, :], 1.0, float(NODES), ALU.is_equal, ALU.mult)\
                .then_inc(edge_step, 1)
            nc.vector.tensor_scalar(known[:, :], rel_i[:, :], 0.0, None, ALU.is_equal).then_inc(edge_step, 1)
            dve.wait_ge(edge_step, 4)
            nc.vector.tensor_tensor(msg_idx[:, :], msg_idx[:, :], src_idx[:, :], ALU.add).then_inc(edge_step, 1)
            nc.vector.scalar_tensor_tensor(out=known[:, :], in0=rel_i[:, :], scalar=1.0, in1=known[:, :],
                                           op0=ALU.is_equal, op1=ALU.add).then_inc(edge_step, 1)
            dve.wait_ge(starts_ready, 1)
            nc.vector.tensor_tensor(dst_off[:, :], dst_f[:, :], ps_a[:, 0:COLS], ALU.subtract).then_inc(edge_step, 1)
            nc.vector.tensor_tensor(far[:, :], ps_a[:, ROUND + MARGIN:COLS - MARGIN:ROUND], final_cols[:, :],
                                    ALU.is_lt).then_inc(edge_step, 1)
            dve.wait_ge(seq_in, 16)
            nc.vector.tensor_copy(seq_f[:, :], seq_i[:, :]).then_inc(edge_step, 1)
            dve.wait_ge(edge_step, 9)
            nc.vector.tensor_reduce(flags[:, 0:1], far[:, :], AX_X, ALU.add).then_inc(edge_step, 1)
            nc.vector.tensor_reduce(flags[:, 1:2], dst_off[:, 0:TILES], AX_X, ALU.max).then_inc(edge_step, 1)
            nc.vector.tensor_tensor(steps[:, :], seq_f[:, 1:TILES + 1], seq_f[:, 0:TILES], ALU.is_lt)\
                .then_inc(edge_step, 1)
            dve.wait_ge(edge_step, 12)
            nc.vector.tensor_scalar(flags[:, 1:2], flags[:, 1:2], float(SPAN - 1), None, ALU.is_gt)\
                .then_inc(edge_step, 1)
            nc.vector.tensor_reduce(flags[:, 2:3], steps[:, :], AX_X, ALU.add).then_inc(edge_step, 1)
            dve.wait_ge(edge_step, 14)
            nc.vector.tensor_reduce(flag_sum[:, :], flags[:, 0:3], AX_X, ALU.add).then_inc(flags_ready, 1)
            dve.wait_ge(disorder_summed, 1)
            nc.vector.tensor_copy(disorder[:, :], ps_b[:, 0:1]).then_inc(path_ready, 1)

            def group_scale(g):
                a, b = g * GC, (g + 1) * GC
                dve.wait_ge(group_std, g + 1)
                nc.vector.reciprocal(rstd[:, a:b], std[:, a:b]).then_inc(group_rstd, 1)
                dve.wait_ge(group_rstd, g + 1)
                nc.vector.scalar_tensor_tensor(out=shift[:, a:b], in0=mean_var[:, a:b, 0], scalar=-1.0,
                                               in1=rstd[:, a:b], op0=ALU.mult, op1=ALU.mult)\
                    .then_inc(group_shift, 1)

            for g in range(GROUPS):
                dve.wait_ge(x_in[g], 16)
                for c in range(g * GC, (g + 1) * GC):
                    nc.vector.bn_stats(bn[:, c, :], nodes[:, c * D:(c + 1) * D]).then_inc(group_bn, 1)
                dve.wait_ge(group_bn, (g + 1) * GC)
                for c in range(g * GC, (g + 1) * GC):
                    last = nc.vector.bn_aggr(mean_var[:, c, :], bn[:, c, :])
                last.then_inc(group_stats, 1)
                if g > 0:
                    group_scale(g - 1)
            group_scale(GROUPS - 1)

            def build_block(p, b, half):
                value = known if p == 2 else weight
                cols = bass.ds(b * BLOCK, BLOCK)
                if p > 0 or not isinstance(b, int) or b > 0:
                    dve.wait_ge(sel_ready, b + BLOCKS * p)
                nc.vector.tensor_tensor(one_hot, iota_cols,
                                        dst_off[:, cols].unsqueeze(2).to_broadcast([P, BLOCK, SPAN]),
                                        ALU.is_equal).then_inc(hot_ready, 1)
                dve.wait_ge(hot_ready, b + (BLOCKS * p + 1))
                nc.vector.tensor_tensor(sel[:, half * BLOCK:(half + 1) * BLOCK, :], one_hot,
                                        value[:, cols].unsqueeze(2).to_broadcast([P, BLOCK, SPAN]),
                                        ALU.mult).then_inc(sel_ready, 1)

            def first_destinations(b):
                _, starts = nc.values_load_multi_w_load_instructions(
                    dst_i[0:1, bass.ds(b * BLOCK, BLOCK)], engines=[dve.engine], min_val=0,
                    max_val=N_NODES - 1, skip_runtime_bounds_check_because="destinations are nodes")
                return starts

            def add_tile(p, i, s, start):
                dve.wait_ge(product_done, i * ROUND + (TILES * p + s + 1))
                if p > 0 or s > 0 or not isinstance(i, int) or i > 0:
                    dve.wait_ge(added, i * ROUND + (TILES * p + s))
                window = acc[:, :, bass.ds(start, SPAN)]
                own = (s % SIDE) * SPAN
                nc.vector.tensor_tensor(window, pair(tile_ps[s % BANKS])[:, :, own:own + SPAN], window, ALU.add)\
                    .then_inc(added, 1)

            def residual(c):
                dve.wait_ge(dense_done, c + (CHUNKS + 1))
                nc.vector.tensor_tensor(chunk_nodes(c), ps_a[:, 0:D], chunk_nodes(c), ALU.add).then_inc(x2_ready, 1)
                dve.wait_ge(x2_ready, c + 1)
                settle(dve)
                nc.vector.bn_stats(bn[:, 0, :], chunk_nodes(c)).then_inc(bn_ready, 1)
                dve.wait_ge(bn_ready, c + 1)
                settle(dve)
                nc.vector.bn_aggr(mean_var[:, 0, :], bn[:, 0, :]).then_inc(stats_ready, 1)

            def norm_scale(c):
                dve.wait_ge(std_ready, c + 1)
                nc.vector.reciprocal(rstd[:, 0:1], std[:, 0:1]).then_inc(rstd_ready, 1)
                dve.wait_ge(rstd_ready, c + 1)
                nc.vector.scalar_tensor_tensor(out=shift[:, 0:1], in0=mean_var[:, 0, 0:1], scalar=-1.0,
                                               in1=rstd[:, 0:1], op0=ALU.mult, op1=ALU.mult)\
                    .then_inc(shift_ready, 1)

            def cell_state(c):
                dve.wait_ge(gates_ready, c + 1)
                nc.vector.tensor_tensor(cell[:], gate_i[:], gate_g[:], ALU.mult).then_inc(cell_ready, 1)

            def lstm_out(c):
                dve.wait_ge(cell_tanh_ready, c + 1)
                nc.vector.tensor_tensor(lstm_t[:], gate_o[:], cell_tanh[:], ALU.mult).then_inc(lstm_ready, 1)

            def result(c):
                dve.wait_ge(mlp3_done, c + 1)
                if isinstance(c, int) and c == CHUNKS - 1:
                    y = out_rows[1][:, 0, :]
                else:
                    y = out_rows[0][:, 0, :]
                    if not isinstance(c, int) or c > 0:
                        dve.wait_ge(y_stored, c * 16)
                nc.vector.tensor_tensor(y, ps_b[:, 0:D], chunk_nodes(c), ALU.add).then_inc(y_ready, 1)

            def chunk_step(p, c, s):
                if p == 1:
                    if s == 9:
                        residual(c)
                    if s == 10:
                        norm_scale(c)
                if p == 2:
                    if s == 10:
                        cell_state(c)
                    if s == 11:
                        lstm_out(c)
                    if s == 15:
                        result(c)

            def round_(p, i, chunk, tiles):
                for s in range(tiles):
                    if s == 0:
                        starts = first_destinations(2 * i)
                        if tiles == ROUND:
                            build_block(p, 2 * i + 1, 1)
                    if s == BLOCK:
                        starts = first_destinations(2 * i + 1)
                        build_block(p, 2 * i + 2, 0)
                    add_tile(p, i, s, starts[s % BLOCK])
                    if chunk is not None:
                        chunk_step(p, chunk, s)

            dve.wait_ge(weights_in, 16 * WEIGHTS)
            nc.vector.tensor_tensor(b_gate[:, :], b_ih[:, :], b_hh[:, :], ALU.add).then_inc(bias_ready, 1)

            dve.wait_ge(iota_ready, BLOCK + 1)
            dve.wait_ge(const_made, 4)
            disordered = path(dve)
            with dve.If(disordered == 0):
                for p in range(PROPS):
                    if p > 0:
                        dve.wait_ge(acc_cleared, CHUNKS * p)
                    build_block(p, 0, 0)
                    round_(p, 0, None, ROUND)
                    with dve.Fori(1, ROUNDS) as i:
                        round_(p, i, i - 1, ROUND)
                    round_(p, ROUNDS, None, TAIL)
                    for c in (CHUNKS - 2, CHUNKS - 1):
                        for s in range(ROUND):
                            chunk_step(p, c, s)
            with dve.Else():
                for p in range(PROPS):
                    value = known if p == 2 else weight
                    if p > 0:
                        dve.wait_ge(acc_cleared, CHUNKS * p)
                    with dve.Fori(0, TILES) as j:
                        with dve.Fori(0, CHUNKS) as w:
                            done = (j + TILES * p) * CHUNKS + w + 1
                            nc.vector.tensor_scalar(sel_wide[:, :], iota_f[:, bass.ds(w * P, P)],
                                                    dst_f[:, bass.ds(j, 1)], value[:, bass.ds(j, 1)],
                                                    ALU.is_equal, ALU.mult).then_inc(wide_sel, 1)
                            dve.wait_ge(wide_product, done)
                            nc.vector.tensor_tensor(chunk_cols(w), pair(tile_ps[0]), chunk_cols(w), ALU.add)\
                                .then_inc(wide_added, 1)
                            dve.wait_ge(wide_added, done)
                    if p > 0:
                        for s in range(ROUND):
                            chunk_step(p, 0, s)
                        with dve.Fori(1, CHUNKS - 1) as c:
                            for s in range(ROUND):
                                chunk_step(p, c, s)
                        for s in range(ROUND):
                            chunk_step(p, CHUNKS - 1, s)

        @block.scalar
        def _(act):
            act.wait_ge(const_made, 4)
            for g in range(GROUPS):
                a, b = g * GC, (g + 1) * GC
                act.wait_ge(group_stats, g + 1)
                nc.scalar.activation(std[:, a:b], mean_var[:, a:b, 1], ACT.Sqrt, bias=eps[:, 0:1])\
                    .then_inc(group_std, 1)
                act.wait_ge(group_shift, g + 1)
                buf = (g % 3) * GC
                if g >= 3:
                    act.wait_ge(hidden_stored[g - 3], 16)
                for c in range(a, b):
                    last = nc.scalar.activation(rows[:, buf + c - a, :], nodes[:, c * D:(c + 1) * D], ACT.Relu,
                                                bias=shift[:, c:c + 1], scale=rstd[:, c:c + 1])
                last.then_inc(group_hidden, 1)
                act.wait_ge(group_hidden, g + 1)
                act.dma_start(table[0].rearrange("(c p) f -> p c f", p=P)[:, a:b, :], rows[:, buf:buf + GC, :])\
                    .then_inc(hidden_stored[g], 16)
            act.wait_ge(weights_in, 16 * WEIGHTS)
            act.wait_ge(bias_ready, 1)

            def take_sums(p, c, n):
                nc.scalar.activation(sums[:], chunk_cols(c), ACT.Copy).then_inc(sums_ready, 1)
                if p < PROPS - 1:
                    act.wait_ge(sums_ready, n + 1)
                    settle(act)
                    nc.scalar.activation(chunk_cols(c), zeros[:], ACT.Copy).then_inc(acc_cleared, 1)

            def mid_rows(c, last):
                y = out_rows[last][:, 0, :]
                act.wait_ge(dense_done, c + 1)
                nc.scalar.activation(y, ps_a[:, 0:D], ACT.Copy).then_inc(rows_ready, 1)
                act.wait_ge(rows_ready, c + 1)
                act.dma_start(table[1][bass.ds(c * P, P), :], y).then_inc(table_stored[1], 16)
                if not last:
                    act.wait_ge(table_stored[1], (c + 1) * 16)

            def messages(c, last):
                act.wait_ge(stats_ready, c + 1)
                nc.scalar.activation(std[:, 0:1], mean_var[:, 0, 1:2], ACT.Sqrt, bias=eps[:, 0:1])\
                    .then_inc(std_ready, 1)
                act.wait_ge(shift_ready, c + 1)
                settle(act)
                nc.scalar.activation(hidden[:, :], chunk_nodes(c), ACT.Relu, bias=shift[:, 0:1],
                                     scale=rstd[:, 0:1]).then_inc(hidden_ready, 1)
                act.wait_ge(turned, c + 1)
                nc.scalar.activation(hidden_t[:], pair(ps_b), ACT.Copy).then_inc(turned_copied, 1)
                act.wait_ge(rel1_done, c + 1)
                for r in range(REL):
                    for m in range(K):
                        n = r * K + m
                        done = nc.scalar.activation(rel1_t[:, r, m, :], ps_c[:, n * P:(n + 1) * P], ACT.Relu,
                                                    bias=b_rel_c[:, n:n + 1])
                done.then_inc(rel1_ready, 1)
                y = out_rows[last]
                act.wait_ge(rel2_done, c + 1)
                nc.scalar.activation(y[:], ps_a[:, :].rearrange("p (r f) -> p r f", r=REL), ACT.Relu)\
                    .then_inc(rows_ready, 1)
                act.wait_ge(rows_ready, c + (CHUNKS + 1))
                act.dma_start(table[2].rearrange("(r n) f -> n r f", r=REL)[bass.ds(c * P, P), :, :], y[:])\
                    .then_inc(table_stored[2], 16)
                if not last:
                    act.wait_ge(table_stored[2], (c + 1) * 16)

            def lstm_mlp(c, last):
                act.wait_ge(dense_done, c + (2 * CHUNKS + 1))
                for ps, off, to, gate, func in ((ps_a, 0, gate_i, 0, ACT.Sigmoid), (ps_a, D, gate_g, 2, ACT.Tanh),
                                                (ps_b, D, gate_o, 3, ACT.Sigmoid)):
                    for m in range(K):
                        done = nc.scalar.activation(to[:, m, :], ps[:, off + m * P:off + (m + 1) * P], func,
                                                    bias=b_gate[:, gate * K + m:gate * K + m + 1])
                done.then_inc(gates_ready, 1)
                act.wait_ge(cell_ready, c + 1)
                nc.scalar.activation(cell_tanh[:], cell[:], ACT.Tanh).then_inc(cell_tanh_ready, 1)
                act.wait_ge(mlp1_done, c + 1)
                nc.scalar.activation(mlp1_t[:, :], ps_c[:, 0:P], ACT.Relu, bias=b1[:, 0:1]).then_inc(mlp1_ready, 1)
                act.wait_ge(mlp2_done, c + 1)
                nc.scalar.activation(mlp2_t[:, :], ps_c[:, P:2 * P], ACT.Relu, bias=b2[:, 0:1])\
                    .then_inc(mlp2_ready, 1)
                act.wait_ge(y_ready, c + 1)
                if last:
                    act.dma_start(out[(CHUNKS - 1) * P:N_NODES, :], out_rows[1][0:LAST_ROWS, 0, :])\
                        .then_inc(y_stored, 16)
                else:
                    act.dma_start(out[bass.ds(c * P, P), :], out_rows[0][:, 0, :]).then_inc(y_stored, 16)

            def chunk(p, c, last):
                take_sums(p, c, c + CHUNKS * p)
                (mid_rows, messages, lstm_mlp)[p](c, last)

            disordered = path(act)
            with act.If(disordered == 0):
                for p in range(PROPS):
                    with act.Fori(0, ROUNDS - 1) as c:
                        act.wait_ge(added, c * ROUND + (TILES * p + ROUND + MARGIN))
                        settle(act)
                        chunk(p, c, False)
                    act.wait_ge(added, TILES * (p + 1))
                    chunk(p, CHUNKS - 2, False)
                    chunk(p, CHUNKS - 1, True)
            with act.Else():
                for p in range(PROPS):
                    act.wait_ge(wide_added, TILES * CHUNKS * (p + 1))
                    with act.Fori(0, CHUNKS - 1) as c:
                        chunk(p, c, False)
                    chunk(p, CHUNKS - 1, True)

        @block.tensor
        def _(pe):
            pe.wait_ge(const_made, 4)
            pe.wait_ge(edge_step, 1)
            nc.tensor.matmul(ps_a[:, 0:COLS], ones[0:1, :], dst_f[0:1, :], start=True, stop=True)\
                .then_inc(starts_ready, 1)
            pe.wait_ge(flags_ready, 1)
            nc.tensor.matmul(ps_b[:, 0:1], ones[:, :], flag_sum[:, :], start=True, stop=True)\
                .then_inc(disorder_summed, 1)
            pe.wait_ge(identity_made, 1)
            pe.wait_ge(weights_in, 16 * WEIGHTS)

            def tile(p, i, s):
                j = i * ROUND + (TILES * p + s)
                if s % BLOCK == 0:
                    pe.wait_ge(sel_ready, 2 * i + (BLOCKS * p + s // BLOCK + 1))
                uses = ROUNDS + (1 if s < TAIL else 0)
                pe.wait_ge(gathered[s], (i + (uses * p + 1)) * 16)
                if p > 0 or s >= BANKS or not isinstance(i, int) or i > 0:
                    pe.wait_ge(added, j - (BANKS - 1))
                side = s - s % SIDE
                for k in range(K):
                    last = nc.tensor.matmul(tile_ps[s % BANKS][:, k * P:(k + 1) * P], rows[:, s, k * P:(k + 1) * P],
                                            sel[:, side:side + SIDE, :], start=True, stop=True)
                last.then_inc(product_done, 1)

            def apply(c, p):
                pe.wait_ge(sums_ready, c + (CHUNKS * p + 1))
                for k in range(K):
                    last = nc.tensor.matmul(ps_a[:, 0:D], sums[:, k, :], w_prop[p][:, k, :], start=(k == 0),
                                            stop=(k == K - 1))
                last.then_inc(dense_done, 1)

            def turn(c):
                pe.wait_ge(hidden_ready, c + 1)
                for k in range(K):
                    last = nc.tensor.transpose(ps_b[:, k * P:(k + 1) * P], hidden[:, k * P:(k + 1) * P],
                                               identity[:, :])
                last.then_inc(turned, 1)

            def rel_first(c):
                pe.wait_ge(turned_copied, c + 1)
                for r in range(REL):
                    for m in range(K):
                        n = r * K + m
                        for k in range(K):
                            last = nc.tensor.matmul(ps_c[:, n * P:(n + 1) * P], w_rel[:, r, k, m * P:(m + 1) * P],
                                                    hidden_t[:, k, :], start=(k == 0), stop=(k == K - 1))
                last.then_inc(rel1_done, 1)

            def rel_second(c):
                pe.wait_ge(rel1_ready, c + 1)
                for r in range(REL):
                    cols = ps_a[:, r * D:(r + 1) * D]
                    for k in range(K):
                        nc.tensor.matmul(cols, rel1_t[:, r, k, :], w_rel[:, r, k, :], start=(k == 0), stop=False)
                    last = nc.tensor.matmul(cols, ones[0:1, :], b_rel_r[0:1, r * D:(r + 1) * D], start=False,
                                            stop=True)
                last.then_inc(rel2_done, 1)

            def gates(c):
                pe.wait_ge(sums_ready, c + (2 * CHUNKS + 1))
                for ps, off, gate in ((ps_a, 0, 0), (ps_a, D, 2), (ps_b, D, 3)):
                    for m in range(K):
                        col = gate * D + m * P
                        for k in range(K):
                            last = nc.tensor.matmul(ps[:, off + m * P:off + (m + 1) * P], w_ih[:, k, col:col + P],
                                                    sums[:, k, :], start=(k == 0), stop=(k == K - 1))
                last.then_inc(dense_done, 1)

            def mlp_first(c):
                pe.wait_ge(lstm_ready, c + 1)
                for k in range(K):
                    last = nc.tensor.matmul(ps_c[:, 0:P], w1[:, k, :], lstm_t[:, k, :], start=(k == 0),
                                            stop=(k == K - 1))
                last.then_inc(mlp1_done, 1)

            def mlp_second(c):
                pe.wait_ge(mlp1_ready, c + 1)
                nc.tensor.matmul(ps_c[:, P:2 * P], w2[:, :], mlp1_t[:, :], start=True, stop=True)\
                    .then_inc(mlp2_done, 1)

            def mlp_third(c):
                pe.wait_ge(mlp2_ready, c + 1)
                nc.tensor.matmul(ps_b[:, 0:D], mlp2_t[:, :], w3[:, :], start=True, stop=False)
                nc.tensor.matmul(ps_b[:, 0:D], ones[0:1, :], b3[0:1, :], start=False, stop=True)\
                    .then_inc(mlp3_done, 1)

            def chunk_step(p, c, s):
                if p < 2 and s == 8:
                    apply(c, p)
                if p == 1:
                    if s == 12:
                        turn(c)
                    if s == 13:
                        rel_first(c)
                    if s == 15:
                        rel_second(c)
                if p == 2:
                    if s == 8:
                        gates(c)
                    if s == 12:
                        mlp_first(c)
                    if s == 13:
                        mlp_second(c)
                    if s == 14:
                        mlp_third(c)

            def round_(p, i, chunk, tiles):
                for s in range(tiles):
                    tile(p, i, s)
                    if chunk is not None:
                        chunk_step(p, chunk, s)

            disordered = path(pe)
            with pe.If(disordered == 0):
                for p in range(PROPS):
                    round_(p, 0, None, ROUND)
                    with pe.Fori(1, ROUNDS) as i:
                        round_(p, i, i - 1, ROUND)
                    round_(p, ROUNDS, None, TAIL)
                    for c in (CHUNKS - 2, CHUNKS - 1):
                        for s in range(ROUND):
                            chunk_step(p, c, s)
            with pe.Else():
                for p in range(PROPS):
                    with pe.Fori(0, TILES) as j:
                        pe.wait_ge(wide_gathered, (j + (TILES * p + 1)) * 16)
                        settle(pe)
                        with pe.Fori(0, CHUNKS) as w:
                            pe.wait_ge(wide_sel, (j + TILES * p) * CHUNKS + w + 1)
                            for k in range(K):
                                last = nc.tensor.matmul(tile_ps[0][:, k * P:(k + 1) * P],
                                                        rows[:, 0, k * P:(k + 1) * P], sel_wide[:, :],
                                                        start=True, stop=True)
                            last.then_inc(wide_product, 1)
                    with pe.Fori(0, CHUNKS) as c:
                        for s in range(ROUND):
                            chunk_step(p, c, s)


def kernel(x, src, dst, edge_type_2, edge_weight, L0_gnn_W1, L0_gnn_W2, L1_gnn_W_rel, L1_gnn_b_rel, L1_gnn_W_ih,
           L1_gnn_b_ih, L1_gnn_b_hh, L1_gnn_W1, L1_gnn_b1, L1_gnn_W2, L1_gnn_b2, L1_gnn_W3, L1_gnn_b3):
    import concourse.bacc as bacc
    from concourse.bass_utils import run_bass_kernel_spmd

    def tiled(a, fill):
        a = np.asarray(a)
        return np.ascontiguousarray(
            np.concatenate([a, np.full(COLS * P - N_EDGES, fill, a.dtype)]).reshape(COLS, P).T)

    def halves(a):
        return np.ascontiguousarray(a.reshape(K, P, a.shape[1]).transpose(1, 0, 2))

    def cols(a):
        return np.ascontiguousarray(np.asarray(a).reshape(-1, P).T)

    x = np.asarray(x)
    dst = np.asarray(dst)
    w_rel = np.asarray(L1_gnn_W_rel)
    in_order = np.concatenate([dst, np.full(TILES * (P + 1) - N_EDGES, N_NODES - 1, dst.dtype)])
    arrays = {
        "x": np.concatenate([x, np.zeros((NODES - N_NODES, D), x.dtype)]),
        "src_t": tiled(src, 0),
        "dst_t": tiled(dst, N_NODES - 1),
        "dst_seq": np.ascontiguousarray(np.concatenate(
            [in_order[:P * TILES].reshape(P, TILES), in_order[TILES:].reshape(P, TILES)[:, 0:1]], axis=1)),
        "rel_t": tiled(edge_type_2, PAD_REL),
        "weight_t": tiled(edge_weight, 0),
        "w_prop1": halves(np.asarray(L0_gnn_W1)),
        "w_prop2": halves(np.asarray(L0_gnn_W2)),
        "w_rel_t": np.ascontiguousarray(w_rel.transpose(0, 2, 1).reshape(REL, K, P, D).transpose(2, 0, 1, 3)),
        "b_rel_cols": cols(L1_gnn_b_rel),
        "b_rel_row": np.asarray(L1_gnn_b_rel).reshape(1, REL * D),
        "w_ih_t": halves(np.ascontiguousarray(np.asarray(L1_gnn_W_ih).T)),
        "b_ih_cols": cols(L1_gnn_b_ih),
        "b_hh_cols": cols(L1_gnn_b_hh),
        "w_mlp1": halves(np.ascontiguousarray(np.asarray(L1_gnn_W1).T)),
        "b_mlp1": cols(L1_gnn_b1),
        "w_mlp2": np.ascontiguousarray(np.asarray(L1_gnn_W2).T),
        "b_mlp2": cols(L1_gnn_b2),
        "w_mlp3": np.ascontiguousarray(np.asarray(L1_gnn_W3).T),
        "b_mlp3": np.asarray(L1_gnn_b3).reshape(1, D),
    }
    nc = bacc.Bacc("TRN2", target_bir_lowering=False, num_devices=1)
    args = [nc.dram_tensor(name, a.shape, mybir.dt.from_np(a.dtype), kind="ExternalInput").ap()
            for name, a in arrays.items()]
    out = nc.dram_tensor("out", (N_NODES, D), F32, kind="ExternalOutput").ap()
    build(nc, *args, out)
    return run_bass_kernel_spmd(nc, [arrays], core_ids=[0]).results[0]["out"]
```

```python
from contextlib import ExitStack

import numpy as np

import concourse.bass as bass
from concourse import mybir

F32 = mybir.dt.float32
I32 = mybir.dt.int32
ALU = mybir.AluOpType
ACT = mybir.ActivationFunctionType
AX_X = mybir.AxisListType.X

P = 128
N_NODES = 3125
N_EDGES = 50000
D = 256
K = D // P
CHUNKS = -(-N_NODES // P)
NODES = CHUNKS * P
LAST_ROWS = N_NODES - (CHUNKS - 1) * P
TILES = -(-N_EDGES // P)
BLOCK = 8
BLOCKS = -(-TILES // BLOCK)
COLS = BLOCKS * BLOCK
ROUND = 2 * BLOCK
ROUNDS = TILES // ROUND
TAIL = TILES - ROUNDS * ROUND
SPAN = 32
SIDE = P // SPAN
MARGIN = BLOCK
LAST_MARGIN = 4
BANKS = 4
PROPS = 3
REL = 2
HALF = D // 2
EPS = 1e-5
GROUPS = 5
GC = CHUNKS // GROUPS
SHARES = (0, 1, 1, 1, 2)
GATES = 3
PAD_REL = REL


def build(nc, x, src_t, dst_t, dst_seq, rel_t, weight_t, w_prop1, w_prop2, w_rel_t, b_rel_cols, b_rel_row,
          w_ih_t, b_ih_cols, b_hh_cols, w_mlp1, b_mlp1, w_mlp2, b_mlp2, w_mlp3, b_mlp3, out):
    with ExitStack() as ctx:
        def sb(name, shape, dt=F32):
            return ctx.enter_context(nc.sbuf_tensor(name, shape, dt))

        def bank(name):
            return ctx.enter_context(nc.psum_tensor(name, [P, 512], F32))

        def sem(name):
            return ctx.enter_context(nc.semaphore(name))

        table = [nc.dram_tensor("table_hidden", (NODES, D), F32, kind="Internal").ap(),
                 nc.dram_tensor("table_mid", (N_NODES, D), F32, kind="Internal").ap(),
                 nc.dram_tensor("table_messages", (REL * N_NODES, D), F32, kind="Internal").ap()]

        nodes = sb("nodes", [P, CHUNKS * D])
        acc = sb("acc", [P, K, NODES])
        rows = sb("rows", [P, ROUND, D])
        src_idx = sb("src_idx", [P, COLS], I32)
        msg_idx = sb("msg_idx", [P, COLS], I32)
        dst_i = sb("dst_i", [P, COLS], I32)
        rel_i = sb("rel_i", [P, COLS], I32)
        weight = sb("weight", [P, COLS])
        known = sb("known", [P, COLS])
        dst_f = sb("dst_f", [P, COLS])
        dst_off = sb("dst_off", [P, COLS])
        seq_i = sb("seq_i", [P, TILES + 1], I32)
        seq_f = sb("seq_f", [P, TILES + 1])
        steps = sb("steps", [P, TILES])
        idx_stage = sb("idx_stage", [P, ROUND], I32)
        sel = sb("sel", [P, ROUND, SPAN])
        sel_wide = sb("sel_wide", [P, P])
        window_i = sb("window_i", [P, BLOCK, SPAN], I32)
        iota_i = sb("iota_i", [P, NODES], I32)
        iota_f = sb("iota_f", [P, NODES])
        final_cols = sb("final_cols", [P, ROUNDS])
        final_i = sb("final_i", [P, ROUNDS], I32)
        zeros = sb("zeros", [P, K, P])
        ones = sb("ones", [P, P])
        identity = sb("identity", [P, P])
        eps = sb("eps", [P, 1])
        first_root = sb("first_root", [P, 1])
        flags = sb("flags", [P, 4])
        flag_sum = sb("flag_sum", [P, 1])
        far = sb("far", [P, ROUNDS])
        disorder = sb("disorder", [P, 1], I32)

        w_prop = [sb("w_prop1_sb", [P, K, D]), sb("w_prop2_sb", [P, K, D])]
        w_rel = sb("w_rel_sb", [P, REL, K, D])
        b_rel_c = sb("b_rel_c", [P, REL * K])
        b_rel_r = sb("b_rel_r", [1, REL * D])
        w_ih = sb("w_ih_sb", [P, K, 4 * D])
        b_ih = sb("b_ih_sb", [P, 4 * K])
        b_hh = sb("b_hh_sb", [P, 4 * K])
        b_gate = sb("b_gate", [P, 4 * K])
        w1 = sb("w1_sb", [P, K, HALF])
        b1 = sb("b1_sb", [HALF, 1])
        w2 = sb("w2_sb", [HALF, HALF])
        b2 = sb("b2_sb", [HALF, 1])
        w3 = sb("w3_sb", [HALF, D])
        b3 = sb("b3_sb", [1, D])

        def two(name, shape):
            return [sb(f"{name}{v}", shape) for v in range(2)]

        sums = sb("sums", [P, K, P])
        out_rows = two("out_rows", [P, REL, D])
        bn = sb("bn", [P, CHUNKS, 6])
        mean_var = sb("mean_var", [P, CHUNKS, 2])
        std = sb("std", [P, CHUNKS])
        rstd = sb("rstd", [P, CHUNKS])
        shift = sb("shift", [P, CHUNKS])
        centred = sb("centred", [P, D])
        hidden = two("hidden", [P, D])
        hidden_t = two("hidden_t", [P, K, P])
        rel1_t = two("rel1_t", [P, REL, K, P])
        gate_i = two("gate_i", [P, K, P])
        gate_g = two("gate_g", [P, K, P])
        gate_o = two("gate_o", [P, K, P])
        cell = two("cell", [P, K, P])
        cell_tanh = two("cell_tanh", [P, K, P])
        lstm_t = two("lstm_t", [P, K, P])
        mlp1_t = two("mlp1_t", [HALF, P])
        mlp2_t = two("mlp2_t", [HALF, P])

        tile_ps = [bank(f"tile_ps{i}") for i in range(BANKS)]
        iota_ps = bank("iota_ps")
        ps_a, ps_b, ps_c = ([bank(f"ps_{n}"), tile_ps[i]] for i, n in enumerate("abc"))
        iota_cols = iota_ps[:, 0:BLOCK * SPAN].rearrange("p (t n) -> p t n", n=SPAN)
        one_hot = iota_ps[:, BLOCK * SPAN:2 * BLOCK * SPAN].rearrange("p (t n) -> p t n", n=SPAN)

        dst_in, seq_in, edges_in, weights_in = sem("dst_in"), sem("seq_in"), sem("edges_in"), sem("weights_in")
        x_in = [sem(f"x_in{g}") for g in range(GROUPS)]
        iota_made, wide_iota_made, const_made, zero_made, identity_made = (
            sem("iota_made"), sem("wide_iota_made"), sem("const_made"), sem("zero_made"), sem("identity_made"))
        eps_made = sem("eps_made")
        settled = sem("settled")
        iota_ready, wide_iota_ready, bias_ready = sem("iota_ready"), sem("wide_iota_ready"), sem("bias_ready")
        edge_step, msg_step, msg_ready = sem("edge_step"), sem("msg_step"), sem("msg_ready")
        starts_ready, flags_ready, disorder_summed, path_ready = (
            sem("starts_ready"), sem("flags_ready"), sem("disorder_summed"), sem("path_ready"))
        group_bn, group_stats, group_std, group_rstd, group_shift, group_hidden, group_centred, group_scaled = (
            sem("group_bn"), sem("group_stats"), sem("group_std"), sem("group_rstd"), sem("group_shift"),
            sem("group_hidden"), sem("group_centred"), sem("group_scaled"))
        hidden_stored = [sem(f"hidden_stored{g}") for g in range(GROUPS)]
        table_stored = [sem(f"table_stored{p}") for p in range(PROPS)]
        staged = [sem(f"staged{h}") for h in range(2)]
        gathered = [sem(f"gathered{s}") for s in range(ROUND)]
        hot_ready, sel_ready, product_done, added = (
            sem("hot_ready"), sem("sel_ready"), sem("product_done"), sem("added"))
        wide_staged, wide_gathered, wide_sel, wide_product, wide_added = (
            sem("wide_staged"), sem("wide_gathered"), sem("wide_sel"), sem("wide_product"), sem("wide_added"))
        sums_ready, acc_cleared, dense_done = sem("sums_ready"), sem("acc_cleared"), sem("dense_done")
        rows_ready = sem("rows_ready")
        x2_ready, bn_ready, stats_ready, std_ready, rstd_ready, shift_ready, hidden_ready = (
            sem("x2_ready"), sem("bn_ready"), sem("stats_ready"), sem("std_ready"), sem("rstd_ready"),
            sem("shift_ready"), sem("hidden_ready"))
        turned, turned_copied, rel1_done, rel1_ready, rel2_done = (
            sem("turned"), sem("turned_copied"), sem("rel1_done"), sem("rel1_ready"), sem("rel2_done"))
        gate_done, gates_ready, cell_ready, cell_tanh_ready, lstm_ready = (
            sem("gate_done"), sem("gates_ready"), sem("cell_ready"), sem("cell_tanh_ready"), sem("lstm_ready"))
        mlp1_done, mlp1_ready, mlp2_done, mlp2_ready, mlp3_done, y_ready, y_stored = (
            sem("mlp1_done"), sem("mlp1_ready"), sem("mlp2_done"), sem("mlp2_ready"), sem("mlp3_done"),
            sem("y_ready"), sem("y_stored"))

        WEIGHTS = 14

        def path(eng):
            eng.wait_ge(path_ready, 1)
            return nc.values_load(disorder[0:1, 0:1], engines=[eng.engine], min_val=0, max_val=1 << 20,
                                  skip_runtime_bounds_check_because="a count of flags, never negative")

        def settle(eng):
            eng.sem_inc(settled, 1)

        def chunk_cols(c):
            return acc[:, :, bass.ds(c * P, P)]

        def chunk_nodes(c):
            return nodes[:, bass.ds(c * D, D)]

        def pair(ps):
            return ps[:, 0:K * P].rearrange("p (k n) -> p k n", k=K)

        def is_last(c):
            return isinstance(c, int) and c == CHUNKS - 1

        def work(c):
            return (1, LAST_ROWS) if is_last(c) else (0, P)

        def sums_of(c, k):
            return acc[:, k, (CHUNKS - 1) * P:N_NODES] if is_last(c) else sums[:, k, :]

        block = ctx.enter_context(nc.Block())

        @block.sync
        def _(sp):
            for g in range(GROUPS):
                sp.dma_start(nodes[:, g * GC * D:(g + 1) * GC * D].rearrange("p (c f) -> p c f", f=D),
                             x.rearrange("(c p) f -> p c f", p=P)[:, g * GC:(g + 1) * GC, :]).then_inc(x_in[g], 16)
                if g == 0:
                    sp.dma_start(dst_i[:, :], dst_t).then_inc(dst_in, 16)
            sp.dma_start(seq_i[:, :], dst_seq).then_inc(seq_in, 16)
            for to, of in ((src_idx, src_t), (weight, weight_t), (rel_i, rel_t)):
                sp.dma_start(to[:, :], of).then_inc(edges_in, 16)
            def stage(p, b, half):
                index = msg_idx if p == 2 else src_idx
                sp.dma_start(idx_stage[:, half * BLOCK:(half + 1) * BLOCK],
                             index[:, bass.ds(b * BLOCK, BLOCK)]).then_inc(staged[half], 16)

            sp.wait_ge(edges_in, 48)
            stage(0, 0, 0)
            stage(0, 1, 1)
            for g in range(GROUPS):
                sp.wait_ge(hidden_stored[g], 16)
            for to, of in ((w_prop[0], w_prop1), (w_prop[1], w_prop2), (w_rel, w_rel_t), (b_rel_c, b_rel_cols),
                           (b_rel_r, b_rel_row), (w_ih, w_ih_t), (b_ih, b_ih_cols), (b_hh, b_hh_cols),
                           (w1, w_mlp1), (b1, b_mlp1), (w2, w_mlp2), (b2, b_mlp2), (w3, w_mlp3), (b3, b_mlp3)):
                sp.dma_start(to[:], of).then_inc(weights_in, 16)

            disordered = path(sp)
            with sp.If(disordered == 0):
                for p in range(PROPS):
                    if p > 0:
                        if p == 2:
                            sp.wait_ge(msg_ready, 1)
                        sp.wait_ge(product_done, TILES * p)
                        stage(p, 0, 0)
                        stage(p, 1, 1)
                    with sp.Fori(1, ROUNDS) as i:
                        sp.wait_ge(product_done, TILES * p + i * ROUND - BLOCK)
                        stage(p, 2 * i, 0)
                        sp.wait_ge(product_done, TILES * p + i * ROUND)
                        stage(p, 2 * i + 1, 1)
                    sp.wait_ge(product_done, TILES * p + ROUNDS * ROUND - BLOCK)
                    stage(p, BLOCKS - 1, 0)
            with sp.Else():
                sp.wait_ge(staged[0], 16)
                sp.wait_ge(msg_ready, 1)
                for p in range(PROPS):
                    index = msg_idx if p == 2 else src_idx
                    with sp.Fori(0, TILES) as j:
                        sp.dma_start(idx_stage[:, 0:1], index[:, bass.ds(j, 1)]).then_inc(wide_staged, 16)
                        sp.wait_ge(wide_gathered, (j + (TILES * p + 1)) * 16)
                        settle(sp)
            sp.wait_ge(y_stored, 16 * CHUNKS)

        @block.gpsimd
        def _(pool):
            nc.gpsimd.memset(eps[:, :], EPS).then_inc(eps_made, 1)
            nc.gpsimd.memset(ones[:, :], 1.0).then_inc(const_made, 1)
            nc.gpsimd.iota(window_i[:], pattern=[[0, BLOCK], [1, SPAN]], base=0, channel_multiplier=0)\
                .then_inc(iota_made, 1)
            nc.gpsimd.iota(final_i[:, :], pattern=[[P, ROUNDS]], base=P, channel_multiplier=0)\
                .then_inc(iota_made, 1)
            nc.gpsimd.memset(zeros[:], 0.0).then_inc(const_made, 1)
            nc.gpsimd.memset(identity[:, :], 0.0).then_inc(zero_made, 1)
            nc.gpsimd.memset(acc[:], 0.0).then_inc(const_made, 1)
            pool.wait_ge(zero_made, 1)
            nc.gpsimd.affine_select(out=identity[:, :], in_=identity[:, :], compare_op=ALU.not_equal, fill=1.0,
                                    base=0, pattern=[[-1, P]], channel_multiplier=1).then_inc(identity_made, 1)

            def table_complete(p):
                if p == 0:
                    for g in range(GROUPS):
                        pool.wait_ge(hidden_stored[g], 16)
                else:
                    pool.wait_ge(table_stored[p], 16 * CHUNKS)

            def gather(p, s, out_sem):
                pool.indirect_dma_start(rows[:, s, :], None, table[p][:, :],
                                        bass.IndirectOffsetOnAxis(ap=idx_stage[:, s:s + 1], axis=0))\
                    .then_inc(out_sem, 16)

            def round_(p, i, first, tiles):
                for s in range(tiles):
                    if s % BLOCK == 0:
                        half = s // BLOCK
                        uses = ROUNDS + (1 if half * BLOCK < TAIL else 0)
                        pool.wait_ge(staged[half], (i + (uses * p + 1)) * 16)
                    if s % 4 == 0 and not first:
                        pool.wait_ge(product_done, i * ROUND + (TILES * p - ROUND + min(s + 4, tiles)))
                        settle(pool)
                    gather(p, s, gathered[s])

            disordered = path(pool)
            with pool.If(disordered == 0):
                for p in range(PROPS):
                    table_complete(p)
                    round_(p, 0, True, ROUND)
                    with pool.Fori(1, ROUNDS) as i:
                        round_(p, i, False, ROUND)
                    round_(p, ROUNDS, False, TAIL)
            with pool.Else():
                nc.gpsimd.iota(iota_i[:, :], pattern=[[1, NODES]], base=0, channel_multiplier=0)\
                    .then_inc(wide_iota_made, 1)
                for p in range(PROPS):
                    table_complete(p)
                    with pool.Fori(0, TILES) as j:
                        pool.wait_ge(wide_staged, (j + (TILES * p + 1)) * 16)
                        settle(pool)
                        gather(p, 0, wide_gathered)
                        pool.wait_ge(wide_product, (j + (TILES * p + 1)) * CHUNKS)

        @block.vector
        def _(dve):
            def group_statistics(g):
                dve.wait_ge(x_in[g], 16)
                for c in range(g * GC, (g + 1) * GC):
                    nc.vector.bn_stats(bn[:, c, :], nodes[:, c * D:(c + 1) * D]).then_inc(group_bn, 1)
                dve.wait_ge(group_bn, (g + 1) * GC)
                for c in range(g * GC, (g + 1) * GC):
                    last = nc.vector.bn_aggr(mean_var[:, c, :], bn[:, c, :])
                last.then_inc(group_stats, 1)

            def group_scale(g):
                a, b = g * GC, (g + 1) * GC
                dve.wait_ge(group_std, g + 1)
                nc.vector.reciprocal(rstd[:, a:b], std[:, a:b]).then_inc(group_rstd, 1)
                dve.wait_ge(group_rstd, g + 1)
                nc.vector.scalar_tensor_tensor(out=shift[:, a:b], in0=mean_var[:, a:b, 0], scalar=-1.0,
                                               in1=rstd[:, a:b], op0=ALU.mult, op1=ALU.mult)\
                    .then_inc(group_shift, 1)

            def group_share(g):
                if g >= 3 and SHARES[g]:
                    dve.wait_ge(hidden_stored[g - 3], 16)
                for n in range(SHARES[g]):
                    c = (g + 1) * GC - SHARES[g] + n
                    done = sum(SHARES[:g]) + n
                    if done > 0:
                        dve.wait_ge(group_scaled, done)
                    nc.vector.tensor_scalar(centred[:, :], nodes[:, c * D:(c + 1) * D], mean_var[:, c, 0:1], 0.0,
                                            ALU.subtract, ALU.max).then_inc(group_centred, 1)
                    dve.wait_ge(group_centred, done + 1)
                    nc.vector.tensor_scalar(rows[:, (g % 3) * GC + c - g * GC, :], centred[:, :], rstd[:, c:c + 1],
                                            None, ALU.mult).then_inc(group_scaled, 1)

            group_statistics(0)
            dve.wait_ge(dst_in, 16)
            nc.vector.tensor_copy(dst_f[:, :], dst_i[:, :]).then_inc(edge_step, 1)
            for g in range(1, GROUPS):
                group_statistics(g)
                group_scale(g - 1)
                group_share(g - 1)
            dve.wait_ge(iota_made, 2)
            nc.vector.tensor_copy(final_cols[:, :], final_i[:, :]).then_inc(edge_step, 1)
            nc.vector.tensor_copy(iota_cols, window_i[:]).then_inc(iota_ready, 1)
            group_scale(GROUPS - 1)
            group_share(GROUPS - 1)

            dve.wait_ge(starts_ready, 1)
            nc.vector.tensor_tensor(dst_off[:, :], dst_f[:, :], ps_a[0][:, 0:COLS], ALU.subtract)\
                .then_inc(edge_step, 1)
            dve.wait_ge(seq_in, 16)
            nc.vector.tensor_copy(seq_f[:, :], seq_i[:, :]).then_inc(edge_step, 1)
            dve.wait_ge(edge_step, 2)
            nc.vector.tensor_tensor(far[:, 0:ROUNDS - 1], ps_a[0][:, ROUND + MARGIN:COLS - MARGIN:ROUND],
                                    final_cols[:, 0:ROUNDS - 1], ALU.is_lt).then_inc(edge_step, 1)
            tile = ROUNDS * ROUND + LAST_MARGIN
            nc.vector.tensor_tensor(far[:, ROUNDS - 1:ROUNDS], ps_a[0][:, tile:tile + 1],
                                    final_cols[:, ROUNDS - 1:ROUNDS], ALU.is_lt).then_inc(edge_step, 1)
            dve.wait_ge(edge_step, 4)
            nc.vector.tensor_reduce(flags[:, 1:2], dst_off[:, 0:TILES], AX_X, ALU.max).then_inc(edge_step, 1)
            nc.vector.tensor_tensor(steps[:, :], seq_f[:, 1:TILES + 1], seq_f[:, 0:TILES], ALU.is_lt)\
                .then_inc(edge_step, 1)
            dve.wait_ge(edge_step, 8)
            nc.vector.tensor_reduce(flags[:, 0:1], far[:, :], AX_X, ALU.add).then_inc(edge_step, 1)
            nc.vector.tensor_scalar(flags[:, 1:2], flags[:, 1:2], float(SPAN - 1), None, ALU.is_gt)\
                .then_inc(edge_step, 1)
            nc.vector.tensor_reduce(flags[:, 2:3], steps[:, :], AX_X, ALU.add).then_inc(edge_step, 1)
            dve.wait_ge(edge_step, 11)
            nc.vector.tensor_reduce(flag_sum[:, :], flags[:, 0:3], AX_X, ALU.add).then_inc(flags_ready, 1)
            dve.wait_ge(disorder_summed, 1)
            nc.vector.tensor_copy(disorder[:, :], ps_b[0][:, 0:1]).then_inc(path_ready, 1)

            def message_arrays():
                nc.vector.tensor_scalar(msg_idx[:, :], rel_i[:, :], 1.0, float(N_NODES), ALU.is_equal, ALU.mult)\
                    .then_inc(msg_step, 1)
                nc.vector.tensor_scalar(known[:, :], rel_i[:, :], 0.0, None, ALU.is_equal).then_inc(msg_step, 1)
                dve.wait_ge(msg_step, 2)
                nc.vector.scalar_tensor_tensor(out=known[:, :], in0=rel_i[:, :], scalar=1.0, in1=known[:, :],
                                               op0=ALU.is_equal, op1=ALU.add).then_inc(msg_step, 1)
                nc.vector.tensor_tensor(msg_idx[:, :], msg_idx[:, :], src_idx[:, :], ALU.add).then_inc(msg_ready, 1)
                dve.wait_ge(msg_step, 3)

            def gate_bias():
                dve.wait_ge(weights_in, 16 * WEIGHTS)
                nc.vector.tensor_tensor(b_gate[:, :], b_ih[:, :], b_hh[:, :], ALU.add).then_inc(bias_ready, 1)

            def build_block(p, b, half):
                value = known if p == 2 else weight
                cols = bass.ds(b * BLOCK, BLOCK)
                if p > 0 or not isinstance(b, int) or b > 0:
                    dve.wait_ge(sel_ready, b + BLOCKS * p)
                nc.vector.tensor_tensor(one_hot, iota_cols,
                                        dst_off[:, cols].unsqueeze(2).to_broadcast([P, BLOCK, SPAN]),
                                        ALU.is_equal).then_inc(hot_ready, 1)
                dve.wait_ge(hot_ready, b + (BLOCKS * p + 1))
                nc.vector.tensor_tensor(sel[:, half * BLOCK:(half + 1) * BLOCK, :], one_hot,
                                        value[:, cols].unsqueeze(2).to_broadcast([P, BLOCK, SPAN]),
                                        ALU.mult).then_inc(sel_ready, 1)

            def first_destinations(b):
                _, starts = nc.values_load_multi_w_load_instructions(
                    dst_i[0:1, bass.ds(b * BLOCK, BLOCK)], engines=[dve.engine], min_val=0,
                    max_val=N_NODES - 1, skip_runtime_bounds_check_because="destinations are nodes")
                return starts

            def add_tile(p, i, s, start):
                dve.wait_ge(product_done, i * ROUND + (TILES * p + s + 1))
                if p > 0 or s > 0 or not isinstance(i, int) or i > 0:
                    dve.wait_ge(added, i * ROUND + (TILES * p + s))
                window = acc[:, :, bass.ds(start, SPAN)]
                own = (s % SIDE) * SPAN
                nc.vector.tensor_tensor(window, pair(tile_ps[s % BANKS])[:, :, own:own + SPAN], window, ALU.add)\
                    .then_inc(added, 1)

            def residual(c):
                v, n = work(c)
                x_rows = chunk_nodes(c)[0:n, :]
                dve.wait_ge(dense_done, c + (CHUNKS + 1))
                nc.vector.tensor_tensor(x_rows, ps_a[v][0:n, 0:D], x_rows, ALU.add).then_inc(x2_ready, 1)
                dve.wait_ge(x2_ready, c + 1)
                settle(dve)
                nc.vector.bn_stats(bn[0:n, v, :], x_rows).then_inc(bn_ready, 1)
                dve.wait_ge(bn_ready, c + 1)
                settle(dve)
                nc.vector.bn_aggr(mean_var[0:n, v, :], bn[0:n, v, :]).then_inc(stats_ready, 1)

            def norm_scale(c):
                v, n = work(c)
                dve.wait_ge(std_ready, c + 1)
                nc.vector.reciprocal(rstd[0:n, v:v + 1], std[0:n, v:v + 1]).then_inc(rstd_ready, 1)
                dve.wait_ge(rstd_ready, c + 1)
                nc.vector.scalar_tensor_tensor(out=shift[0:n, v:v + 1], in0=mean_var[0:n, v, 0:1], scalar=-1.0,
                                               in1=rstd[0:n, v:v + 1], op0=ALU.mult, op1=ALU.mult)\
                    .then_inc(shift_ready, 1)

            def cell_state(c):
                v, n = work(c)
                dve.wait_ge(gates_ready, c + 1)
                nc.vector.tensor_tensor(cell[v][:, :, 0:n], gate_i[v][:, :, 0:n], gate_g[v][:, :, 0:n], ALU.mult)\
                    .then_inc(cell_ready, 1)

            def lstm_out(c):
                v, n = work(c)
                dve.wait_ge(cell_tanh_ready, c + 1)
                nc.vector.tensor_tensor(lstm_t[v][:, :, 0:n], gate_o[v][:, :, 0:n], cell_tanh[v][:, :, 0:n],
                                        ALU.mult).then_inc(lstm_ready, 1)

            def result(c):
                v, n = work(c)
                dve.wait_ge(mlp3_done, c + 1)
                if v == 0 and not (isinstance(c, int) and c == 0):
                    dve.wait_ge(y_stored, c * 16)
                nc.vector.tensor_tensor(out_rows[v][0:n, 0, :], ps_c[v][0:n, 0:D],
                                        chunk_nodes(c)[0:n, :], ALU.add).then_inc(y_ready, 1)

            def chunk_step(p, c, s):
                if p == 1:
                    if s == 9:
                        residual(c)
                    if s == 10:
                        norm_scale(c)
                if p == 2:
                    if s == 13:
                        cell_state(c)
                    if s == 14:
                        lstm_out(c)
                    if s == 3:
                        result(c)

            def whole_chunk(p, c):
                for s in (*range(BLOCK, ROUND), *range(BLOCK)):
                    chunk_step(p, c, s)

            def last_chunks(p):
                a, b = CHUNKS - 2, CHUNKS - 1
                if p == 1:
                    residual(a)
                    residual(b)
                    norm_scale(a)
                    norm_scale(b)
                if p == 2:
                    cell_state(a)
                    lstm_out(a)
                    cell_state(b)
                    lstm_out(b)
                    result(a)
                    result(b)

            def round_(p, i, late, early, tiles):
                for s in range(tiles):
                    if s == 0:
                        starts = first_destinations(2 * i)
                        if tiles == ROUND:
                            build_block(p, 2 * i + 1, 1)
                    if s == BLOCK:
                        starts = first_destinations(2 * i + 1)
                        build_block(p, 2 * i + 2, 0)
                    add_tile(p, i, s, starts[s % BLOCK])
                    chunk = late if s < BLOCK else early
                    if chunk is not None:
                        chunk_step(p, chunk, s)

            dve.wait_ge(edges_in, 48)
            dve.wait_ge(iota_ready, 1)
            dve.wait_ge(const_made, 3)
            disordered = path(dve)
            with dve.If(disordered == 0):
                for p in range(PROPS):
                    if p > 0:
                        dve.wait_ge(acc_cleared, CHUNKS * p)
                    build_block(p, 0, 0)
                    round_(p, 0, None, None, ROUND)
                    if p == 0:
                        message_arrays()
                    if p == 1:
                        gate_bias()
                    round_(p, 1, None, 0, ROUND)
                    with dve.Fori(2, ROUNDS) as i:
                        round_(p, i, i - 2, i - 1, ROUND)
                    round_(p, ROUNDS, ROUNDS - 2, None, TAIL)
                    last_chunks(p)
            with dve.Else():
                message_arrays()
                gate_bias()
                dve.wait_ge(wide_iota_made, 1)
                nc.vector.tensor_copy(iota_f[:, :], iota_i[:, :]).then_inc(wide_iota_ready, 1)
                dve.wait_ge(wide_iota_ready, 1)
                for p in range(PROPS):
                    value = known if p == 2 else weight
                    if p > 0:
                        dve.wait_ge(acc_cleared, CHUNKS * p)
                    with dve.Fori(0, TILES) as j:
                        with dve.Fori(0, CHUNKS) as w:
                            done = (j + TILES * p) * CHUNKS + w + 1
                            nc.vector.tensor_scalar(sel_wide[:, :], iota_f[:, bass.ds(w * P, P)],
                                                    dst_f[:, bass.ds(j, 1)], value[:, bass.ds(j, 1)],
                                                    ALU.is_equal, ALU.mult).then_inc(wide_sel, 1)
                            dve.wait_ge(wide_product, done)
                            nc.vector.tensor_tensor(chunk_cols(w), pair(tile_ps[0]), chunk_cols(w), ALU.add)\
                                .then_inc(wide_added, 1)
                            dve.wait_ge(wide_added, done)
                    if p > 0:
                        whole_chunk(p, 0)
                        with dve.Fori(1, CHUNKS - 1) as c:
                            whole_chunk(p, c)
                        whole_chunk(p, CHUNKS - 1)

        @block.scalar
        def _(act):
            act.wait_ge(eps_made, 1)
            nc.scalar.activation(first_root[:, :], eps[:, :], ACT.Sqrt).then_inc(settled, 1)
            def group_deviation(g):
                a, b = g * GC, (g + 1) * GC
                act.wait_ge(group_stats, g + 1)
                nc.scalar.activation(std[:, a:b], mean_var[:, a:b, 1], ACT.Sqrt, bias=eps[:, 0:1])\
                    .then_inc(group_std, 1)

            group_deviation(0)
            for g in range(GROUPS):
                a, b = g * GC, (g + 1) * GC
                if g < GROUPS - 1:
                    group_deviation(g + 1)
                act.wait_ge(group_shift, g + 1)
                buf = (g % 3) * GC
                if g >= 3:
                    act.wait_ge(hidden_stored[g - 3], 16)
                for c in range(a, b - SHARES[g]):
                    last = nc.scalar.activation(rows[:, buf + c - a, :], nodes[:, c * D:(c + 1) * D], ACT.Relu,
                                                bias=shift[:, c:c + 1], scale=rstd[:, c:c + 1])
                last.then_inc(group_hidden, 1)
                act.wait_ge(group_hidden, g + 1)
                if SHARES[g]:
                    act.wait_ge(group_scaled, sum(SHARES[:g + 1]))
                act.dma_start(table[0].rearrange("(c p) f -> p c f", p=P)[:, a:b, :], rows[:, buf:buf + GC, :])\
                    .then_inc(hidden_stored[g], 16)
            act.wait_ge(const_made, 3)

            def take_sums(p, c, n):
                nc.scalar.activation(sums[:], chunk_cols(c), ACT.Copy).then_inc(sums_ready, 1)
                if p < PROPS - 1:
                    act.wait_ge(sums_ready, n + 1)
                    settle(act)
                    nc.scalar.activation(chunk_cols(c), zeros[:], ACT.Copy).then_inc(acc_cleared, 1)

            def clear_last(p):
                if p < PROPS - 1:
                    act.wait_ge(dense_done, CHUNKS * (p + 1))
                    nc.scalar.activation(chunk_cols(CHUNKS - 1), zeros[:], ACT.Copy).then_inc(acc_cleared, 1)

            def buffer_free(p, c):
                if not is_last(c) and not (isinstance(c, int) and c == 0):
                    act.wait_ge(table_stored[p], c * 16)
                    settle(act)

            def mid_rows(c):
                v, n = work(c)
                y = out_rows[v][0:n, 0, :]
                buffer_free(1, c)
                act.wait_ge(dense_done, c + 1)
                settle(act)
                nc.scalar.activation(y, ps_a[v][0:n, 0:D], ACT.Copy).then_inc(rows_ready, 1)
                act.wait_ge(rows_ready, c + 1)
                act.dma_start(table[1][bass.ds(c * P, n), :], y).then_inc(table_stored[1], 16)

            def norm(c):
                v, n = work(c)
                act.wait_ge(stats_ready, c + 1)
                nc.scalar.activation(std[0:n, v:v + 1], mean_var[0:n, v, 1:2], ACT.Sqrt, bias=eps[0:n, 0:1])\
                    .then_inc(std_ready, 1)
                act.wait_ge(shift_ready, c + 1)
                settle(act)
                nc.scalar.activation(hidden[v][0:n, :], chunk_nodes(c)[0:n, :], ACT.Relu, bias=shift[0:n, v:v + 1],
                                     scale=rstd[0:n, v:v + 1]).then_inc(hidden_ready, 1)

            def copy_turned(c):
                v, n = work(c)
                act.wait_ge(turned, c + 1)
                nc.scalar.activation(hidden_t[v][:, :, 0:n], pair(ps_b[v])[:, :, 0:n], ACT.Copy)\
                    .then_inc(turned_copied, 1)

            def rel_first(c):
                v, n = work(c)
                for r, ps in enumerate((ps_c[v], ps_b[v])):
                    act.wait_ge(rel1_done, REL * c + (r + 1))
                    for m in range(K):
                        q = r * K + m
                        done = nc.scalar.activation(rel1_t[v][:, r, m, 0:n], ps[:, m * P:m * P + n], ACT.Relu,
                                                    bias=b_rel_c[:, q:q + 1])
                    done.then_inc(rel1_ready, 1)

            def message_rows(c):
                v, n = work(c)
                buffer_free(2, c)
                for r, ps in enumerate((ps_a[v], ps_c[v])):
                    act.wait_ge(rel2_done, REL * c + (r + 1))
                    settle(act)
                    nc.scalar.activation(out_rows[v][0:n, r, :], ps[0:n, 0:D], ACT.Relu)\
                        .then_inc(rows_ready, 1)
                act.wait_ge(rows_ready, REL * c + (CHUNKS + REL))
                act.dma_start(table[2].rearrange("(r n) f -> n r f", r=REL)[bass.ds(c * P, n), :, :],
                              out_rows[v][0:n, :, :]).then_inc(table_stored[2], 16)

            def gates(c):
                v, n = work(c)
                for t, (ps, to, gate, func) in enumerate((
                        (ps_a, gate_i, 0, ACT.Sigmoid), (ps_b, gate_g, 2, ACT.Tanh),
                        (ps_c, gate_o, 3, ACT.Sigmoid))):
                    act.wait_ge(gate_done, GATES * c + (t + 1))
                    for m in range(K):
                        done = nc.scalar.activation(to[v][:, m, 0:n], ps[v][:, m * P:m * P + n], func,
                                                    bias=b_gate[:, gate * K + m:gate * K + m + 1])
                done.then_inc(gates_ready, 1)

            def tanh_cell(c):
                v, n = work(c)
                act.wait_ge(cell_ready, c + 1)
                nc.scalar.activation(cell_tanh[v][:, :, 0:n], cell[v][:, :, 0:n], ACT.Tanh)\
                    .then_inc(cell_tanh_ready, 1)

            def mlp_first(c):
                v, n = work(c)
                act.wait_ge(mlp1_done, c + 1)
                nc.scalar.activation(mlp1_t[v][:, 0:n], ps_a[v][:, 0:n], ACT.Relu, bias=b1[:, 0:1])\
                    .then_inc(mlp1_ready, 1)

            def mlp_second(c):
                v, n = work(c)
                act.wait_ge(mlp2_done, c + 1)
                nc.scalar.activation(mlp2_t[v][:, 0:n], ps_a[v][:, P:P + n], ACT.Relu, bias=b2[:, 0:1])\
                    .then_inc(mlp2_ready, 1)

            def store_result(c):
                v, n = work(c)
                act.wait_ge(y_ready, c + 1)
                act.dma_start(out[bass.ds(c * P, n), :], out_rows[v][0:n, 0, :]).then_inc(y_stored, 16)

            def chunk(p, c):
                if is_last(c):
                    clear_last(p)
                else:
                    take_sums(p, c, c + (CHUNKS - 1) * p)
                if p == 0:
                    mid_rows(c)
                if p == 1:
                    norm(c)
                    copy_turned(c)
                    rel_first(c)
                    message_rows(c)
                if p == 2:
                    gates(c)
                    tanh_cell(c)
                    mlp_first(c)
                    mlp_second(c)
                    store_result(c)

            def last_chunks(p):
                a, b = CHUNKS - 2, CHUNKS - 1
                take_sums(p, a, a + (CHUNKS - 1) * p)
                if p == 0:
                    mid_rows(a)
                    mid_rows(b)
                    clear_last(p)
                if p == 1:
                    norm(a)
                    copy_turned(a)
                    norm(b)
                    clear_last(p)
                    rel_first(a)
                    copy_turned(b)
                    message_rows(a)
                    rel_first(b)
                    message_rows(b)
                if p == 2:
                    gates(a)
                    tanh_cell(a)
                    gates(b)
                    mlp_first(a)
                    tanh_cell(b)
                    mlp_second(a)
                    mlp_first(b)
                    mlp_second(b)
                    store_result(a)
                    store_result(b)

            disordered = path(act)
            act.wait_ge(weights_in, 16 * WEIGHTS)
            with act.If(disordered == 0):
                for p in range(PROPS):
                    if p == 2:
                        act.wait_ge(bias_ready, 1)
                    act.wait_ge(added, TILES * p + ROUND + MARGIN)
                    chunk(p, 0)
                    with act.Fori(1, ROUNDS - 1) as c:
                        act.wait_ge(added, c * ROUND + (TILES * p + ROUND + MARGIN))
                        settle(act)
                        chunk(p, c)
                    act.wait_ge(added, TILES * p + ROUNDS * ROUND + LAST_MARGIN)
                    last_chunks(p)
            with act.Else():
                for p in range(PROPS):
                    if p == 2:
                        act.wait_ge(bias_ready, 1)
                    act.wait_ge(wide_added, TILES * CHUNKS * (p + 1))
                    chunk(p, 0)
                    with act.Fori(1, CHUNKS - 1) as c:
                        chunk(p, c)
                    chunk(p, CHUNKS - 1)

        @block.tensor
        def _(pe):
            pe.wait_ge(const_made, 1)
            pe.wait_ge(edge_step, 1)
            nc.tensor.matmul(ps_a[0][:, 0:COLS], ones[0:1, :], dst_f[0:1, :], start=True, stop=True)\
                .then_inc(starts_ready, 1)
            pe.wait_ge(flags_ready, 1)
            nc.tensor.matmul(ps_b[0][:, 0:1], ones[:, :], flag_sum[:, :], start=True, stop=True)\
                .then_inc(disorder_summed, 1)
            pe.wait_ge(identity_made, 1)

            def tile(p, i, s):
                j = i * ROUND + (TILES * p + s)
                if s % BLOCK == 0:
                    pe.wait_ge(sel_ready, 2 * i + (BLOCKS * p + s // BLOCK + 1))
                uses = ROUNDS + (1 if s < TAIL else 0)
                pe.wait_ge(gathered[s], (i + (uses * p + 1)) * 16)
                if p > 0 or s >= BANKS or not isinstance(i, int) or i > 0:
                    pe.wait_ge(added, j - (BANKS - 1))
                side = s - s % SIDE
                for k in range(K):
                    last = nc.tensor.matmul(tile_ps[s % BANKS][:, k * P:(k + 1) * P], rows[:, s, k * P:(k + 1) * P],
                                            sel[:, side:side + SIDE, :], start=True, stop=True)
                last.then_inc(product_done, 1)

            def wait_for_sums(c, p):
                if not is_last(c):
                    pe.wait_ge(sums_ready, c + ((CHUNKS - 1) * p + 1))

            def apply(c, p):
                v, n = work(c)
                wait_for_sums(c, p)
                for k in range(K):
                    last = nc.tensor.matmul(ps_a[v][0:n, 0:D], sums_of(c, k), w_prop[p][:, k, :], start=(k == 0),
                                            stop=(k == K - 1))
                last.then_inc(dense_done, 1)

            def turn(c):
                v, n = work(c)
                pe.wait_ge(hidden_ready, c + 1)
                for k in range(K):
                    last = nc.tensor.transpose(ps_b[v][:, k * P:k * P + n], hidden[v][0:n, k * P:(k + 1) * P],
                                               identity[0:n, 0:n])
                last.then_inc(turned, 1)

            def rel_first(c, r):
                v, n = work(c)
                ps = (ps_c[v], ps_b[v])[r]
                if r == 0:
                    pe.wait_ge(turned_copied, c + 1)
                for m in range(K):
                    for k in range(K):
                        last = nc.tensor.matmul(ps[:, m * P:m * P + n], w_rel[:, r, k, m * P:(m + 1) * P],
                                                hidden_t[v][:, k, 0:n], start=(k == 0), stop=(k == K - 1))
                last.then_inc(rel1_done, 1)

            def rel_second(c, r):
                v, n = work(c)
                cols = (ps_a[v], ps_c[v])[r][0:n, 0:D]
                nc.tensor.matmul(cols, ones[0:1, 0:n], b_rel_r[0:1, r * D:(r + 1) * D], start=True, stop=False)
                pe.wait_ge(rel1_ready, REL * c + (r + 1))
                for k in range(K):
                    last = nc.tensor.matmul(cols, rel1_t[v][:, r, k, 0:n], w_rel[:, r, k, :], start=False,
                                            stop=(k == K - 1))
                last.then_inc(rel2_done, 1)

            def gate_product(c, t):
                v, n = work(c)
                ps, gate = ((ps_a[v], 0), (ps_b[v], 2), (ps_c[v], 3))[t]
                if t == 0:
                    wait_for_sums(c, 2)
                for m in range(K):
                    col = gate * D + m * P
                    for k in range(K):
                        last = nc.tensor.matmul(ps[:, m * P:m * P + n], w_ih[:, k, col:col + P],
                                                sums_of(c, k), start=(k == 0), stop=(k == K - 1))
                last.then_inc(gate_done, 1)

            def mlp_first(c):
                v, n = work(c)
                pe.wait_ge(lstm_ready, c + 1)
                for k in range(K):
                    last = nc.tensor.matmul(ps_a[v][:, 0:n], w1[:, k, :], lstm_t[v][:, k, 0:n], start=(k == 0),
                                            stop=(k == K - 1))
                last.then_inc(mlp1_done, 1)

            def mlp_second(c):
                v, n = work(c)
                pe.wait_ge(mlp1_ready, c + 1)
                nc.tensor.matmul(ps_a[v][:, P:P + n], w2[:, :], mlp1_t[v][:, 0:n], start=True, stop=True)\
                    .then_inc(mlp2_done, 1)

            def mlp_third(c):
                v, n = work(c)
                cols = ps_c[v][0:n, 0:D]
                nc.tensor.matmul(cols, ones[0:1, 0:n], b3[0:1, :], start=True, stop=False)
                pe.wait_ge(mlp2_ready, c + 1)
                nc.tensor.matmul(cols, mlp2_t[v][:, 0:n], w3[:, :], start=False, stop=True).then_inc(mlp3_done, 1)

            def chunk_step(p, c, s):
                if p < 2 and s == 8:
                    apply(c, p)
                if p == 1:
                    if s == 12:
                        turn(c)
                    if s == 13:
                        rel_first(c, 0)
                    if s == 15:
                        rel_first(c, 1)
                    if s == 0:
                        rel_second(c, 0)
                    if s == 1:
                        rel_second(c, 1)
                if p == 2:
                    if s == 8:
                        gate_product(c, 0)
                    if s == 10:
                        gate_product(c, 1)
                    if s == 12:
                        gate_product(c, 2)
                    if s == 15:
                        mlp_first(c)
                    if s == 0:
                        mlp_second(c)
                    if s == 1:
                        mlp_third(c)

            def whole_chunk(p, c):
                for s in (*range(BLOCK, ROUND), *range(BLOCK)):
                    chunk_step(p, c, s)

            def tail_step(p, s):
                a = CHUNKS - 2
                if p == 2 and s in (4, 5, 6):
                    gate_product(a, s - 4)

            def last_chunks(p):
                a, b = CHUNKS - 2, CHUNKS - 1
                if p < 2:
                    apply(a, p)
                pe.wait_ge(added, TILES * (p + 1))
                if p == 0:
                    apply(b, p)
                if p == 1:
                    apply(b, p)
                    turn(a)
                    rel_first(a, 0)
                    rel_first(a, 1)
                    turn(b)
                    rel_second(a, 0)
                    rel_second(a, 1)
                    rel_first(b, 0)
                    rel_first(b, 1)
                    rel_second(b, 0)
                    rel_second(b, 1)
                if p == 2:
                    gate_product(b, 0)
                    gate_product(b, 1)
                    gate_product(b, 2)
                    mlp_first(a)
                    mlp_second(a)
                    mlp_third(a)
                    mlp_first(b)
                    mlp_second(b)
                    mlp_third(b)

            def round_(p, i, late, early, tiles):
                for s in range(tiles):
                    tile(p, i, s)
                    chunk = late if s < BLOCK else early
                    if chunk is not None:
                        chunk_step(p, chunk, s)
                    if tiles == TAIL:
                        tail_step(p, s)

            disordered = path(pe)
            with pe.If(disordered == 0):
                for p in range(PROPS):
                    round_(p, 0, None, None, ROUND)
                    if p == 0:
                        pe.wait_ge(weights_in, 16 * WEIGHTS)
                    round_(p, 1, None, 0, ROUND)
                    with pe.Fori(2, ROUNDS) as i:
                        round_(p, i, i - 2, i - 1, ROUND)
                    round_(p, ROUNDS, ROUNDS - 2, None, TAIL)
                    last_chunks(p)
            with pe.Else():
                pe.wait_ge(weights_in, 16 * WEIGHTS)
                for p in range(PROPS):
                    with pe.Fori(0, TILES) as j:
                        pe.wait_ge(wide_gathered, (j + (TILES * p + 1)) * 16)
                        settle(pe)
                        with pe.Fori(0, CHUNKS) as w:
                            pe.wait_ge(wide_sel, (j + TILES * p) * CHUNKS + w + 1)
                            for k in range(K):
                                last = nc.tensor.matmul(tile_ps[0][:, k * P:(k + 1) * P],
                                                        rows[:, 0, k * P:(k + 1) * P], sel_wide[:, :],
                                                        start=True, stop=True)
                            last.then_inc(wide_product, 1)
                    with pe.Fori(0, CHUNKS - 1) as c:
                        whole_chunk(p, c)
                    pe.wait_ge(wide_added, TILES * CHUNKS * (p + 1))
                    whole_chunk(p, CHUNKS - 1)


def kernel(x, src, dst, edge_type_2, edge_weight, L0_gnn_W1, L0_gnn_W2, L1_gnn_W_rel, L1_gnn_b_rel, L1_gnn_W_ih,
           L1_gnn_b_ih, L1_gnn_b_hh, L1_gnn_W1, L1_gnn_b1, L1_gnn_W2, L1_gnn_b2, L1_gnn_W3, L1_gnn_b3):
    import concourse.bacc as bacc
    from concourse.bass_utils import run_bass_kernel_spmd

    def tiled(a, fill):
        a = np.asarray(a)
        return np.ascontiguousarray(
            np.concatenate([a, np.full(COLS * P - N_EDGES, fill, a.dtype)]).reshape(COLS, P).T)

    def halves(a):
        return np.ascontiguousarray(a.reshape(K, P, a.shape[1]).transpose(1, 0, 2))

    def cols(a):
        return np.ascontiguousarray(np.asarray(a).reshape(-1, P).T)

    x = np.asarray(x)
    dst = np.asarray(dst)
    w_rel = np.asarray(L1_gnn_W_rel)
    in_order = np.concatenate([dst, np.full(TILES * (P + 1) - N_EDGES, N_NODES - 1, dst.dtype)])
    arrays = {
        "x": np.concatenate([x, np.zeros((NODES - N_NODES, D), x.dtype)]),
        "src_t": tiled(src, 0),
        "dst_t": tiled(dst, N_NODES - 1),
        "dst_seq": np.ascontiguousarray(np.concatenate(
            [in_order[:P * TILES].reshape(P, TILES), in_order[TILES:].reshape(P, TILES)[:, 0:1]], axis=1)),
        "rel_t": tiled(edge_type_2, PAD_REL),
        "weight_t": tiled(edge_weight, 0),
        "w_prop1": halves(np.asarray(L0_gnn_W1)),
        "w_prop2": halves(np.asarray(L0_gnn_W2)),
        "w_rel_t": np.ascontiguousarray(w_rel.transpose(0, 2, 1).reshape(REL, K, P, D).transpose(2, 0, 1, 3)),
        "b_rel_cols": cols(L1_gnn_b_rel),
        "b_rel_row": np.asarray(L1_gnn_b_rel).reshape(1, REL * D),
        "w_ih_t": halves(np.ascontiguousarray(np.asarray(L1_gnn_W_ih).T)),
        "b_ih_cols": cols(L1_gnn_b_ih),
        "b_hh_cols": cols(L1_gnn_b_hh),
        "w_mlp1": halves(np.ascontiguousarray(np.asarray(L1_gnn_W1).T)),
        "b_mlp1": cols(L1_gnn_b1),
        "w_mlp2": np.ascontiguousarray(np.asarray(L1_gnn_W2).T),
        "b_mlp2": cols(L1_gnn_b2),
        "w_mlp3": np.ascontiguousarray(np.asarray(L1_gnn_W3).T),
        "b_mlp3": np.asarray(L1_gnn_b3).reshape(1, D),
    }
    nc = bacc.Bacc("TRN2", target_bir_lowering=False, num_devices=1)
    args = [nc.dram_tensor(name, a.shape, mybir.dt.from_np(a.dtype), kind="ExternalInput").ap()
            for name, a in arrays.items()]
    out = nc.dram_tensor("out", (N_NODES, D), F32, kind="ExternalOutput").ap()
    build(nc, *args, out)
    return run_bass_kernel_spmd(nc, [arrays], core_ids=[0]).results[0]["out"]
```

```python
from contextlib import ExitStack

import numpy as np

import concourse.bass as bass
from concourse import mybir

F32 = mybir.dt.float32
I32 = mybir.dt.int32
ALU = mybir.AluOpType
ACT = mybir.ActivationFunctionType
AX_X = mybir.AxisListType.X
XY = mybir.AxisListType.XY

P = 128
N_NODES = 3125
N_EDGES = 50000
D = 256
K = D // P
CHUNKS = -(-N_NODES // P)
NODES = CHUNKS * P
LAST_ROWS = N_NODES - (CHUNKS - 1) * P
TILES = -(-N_EDGES // P)
BLOCK = 8
BLOCKS = -(-TILES // BLOCK)
COLS = BLOCKS * BLOCK
ROUND = 2 * BLOCK
ROUNDS = TILES // ROUND
TAIL = TILES - ROUNDS * ROUND
BUILD_AT = 2
SPAN = 32
SIDE = P // SPAN
MARGIN = BLOCK
LAST_MARGIN = 4
BANKS = (2, 4, 4)
PROPS = 3
REL = 2
HALF = D // 2
EPS = 1e-5
GROUPS = 5
GC = CHUNKS // GROUPS
SHARES = (1, 1, 1, 2, 2)
GATES = 3
GATHER_ROUNDS = 20
GATHERED = GATHER_ROUNDS * ROUND
BUILT = COLS - GATHERED
GROUP = 12
BUILD_GROUPS = BUILT // GROUP
GROUP_ROUNDS = 3
AHEAD = 3
NARROW = 16
BUILD_STEPS = tuple(2 + 3 * n // 2 for n in range(GROUP))
APPLY_STEP = 20
APPLY_WIDTH = 2
GROUP_ADD_STEP = 46
SUM_CHUNKS = BUILD_GROUPS * GROUP_ROUNDS
assert BUILD_GROUPS * GROUP == BUILT and BUILD_GROUPS * GROUP_ROUNDS == GATHER_ROUNDS - 2
FIRST_TILE = (0, GATHERED, GATHERED + TILES)
FIRST_BLOCK = (0, GATHERED // BLOCK, GATHERED // BLOCK + BLOCKS)
BUILT_CHUNKS = tuple(range(SUM_CHUNKS + 3, CHUNKS))
LATE_CHUNKS = (*BUILT_CHUNKS, SUM_CHUNKS, SUM_CHUNKS + 1, SUM_CHUNKS + 2)
LATE_STEPS = {**{2 * n: n for n in range(len(BUILT_CHUNKS))}, MARGIN + 1: len(BUILT_CHUNKS)}
PAD_REL = REL


def build(nc, x, src_t, dst_t, dst_seq, rel_t, weight_t, w_prop1, w_prop2, w_rel_t, b_rel_cols, b_rel_row,
          w_ih_t, b_ih_cols, b_hh_cols, w_mlp1, b_mlp1, w_mlp2, b_mlp2, w_mlp3, b_mlp3, out):
    with ExitStack() as ctx:
        def sb(name, shape, dt=F32):
            return ctx.enter_context(nc.sbuf_tensor(name, shape, dt))

        def bank(name):
            return ctx.enter_context(nc.psum_tensor(name, [P, 512], F32))

        def sem(name):
            return ctx.enter_context(nc.semaphore(name))

        table = [nc.dram_tensor("table_hidden", (NODES, D), F32, kind="Internal").ap(),
                 nc.dram_tensor("table_mid", (N_NODES, D), F32, kind="Internal").ap(),
                 nc.dram_tensor("table_messages", (REL * N_NODES, D), F32, kind="Internal").ap()]

        nodes = sb("nodes", [P, CHUNKS * D])
        acc = sb("acc", [P, K, NODES + P])
        hid = sb("hid", [P, CHUNKS, D])
        part = sb("part", [P, CHUNKS, P])
        weighted_lo = sb("weighted_lo", [P, AHEAD, P])
        keyed = sb("keyed", [P, AHEAD, CHUNKS, NARROW])
        row_i = sb("row_i", [P, CHUNKS * NARROW], I32)
        row_f = sb("row_f", [P, CHUNKS * NARROW])
        lo_i = sb("lo_i", [P, BUILT], I32)
        hi_i = sb("hi_i", [P, BUILT], I32)
        lo_f = sb("lo_f", [P, BUILT])
        key = sb("key", [P, BUILT])
        place_f = sb("place_f", [P, BUILD_GROUPS, GROUP])
        group_first = sb("group_first", [P, BUILD_GROUPS])
        place_i = sb("place_i", [P, BUILT], I32)
        rows = sb("rows", [P, ROUND, D])
        src_idx = sb("src_idx", [P, COLS], I32)
        msg_idx = sb("msg_idx", [P, COLS], I32)
        dst_i = sb("dst_i", [P, COLS], I32)
        rel_i = sb("rel_i", [P, COLS], I32)
        weight = sb("weight", [P, COLS])
        known = sb("known", [P, COLS])
        dst_f = sb("dst_f", [P, COLS])
        dst_off = sb("dst_off", [P, COLS])
        seq_i = sb("seq_i", [P, TILES + 1], I32)
        seq_f = sb("seq_f", [P, TILES + 1])
        steps = sb("steps", [P, TILES])
        idx_stage = sb("idx_stage", [P, ROUND], I32)
        sel = sb("sel", [P, ROUND, SPAN])
        sel_wide = sb("sel_wide", [P, P])
        window_i = sb("window_i", [P, BLOCK, SPAN], I32)
        final_cols = sb("final_cols", [P, ROUNDS])
        final_i = sb("final_i", [P, ROUNDS], I32)
        zeros = sb("zeros", [P, K, P])
        ones = sb("ones", [P, P])
        identity = sb("identity", [P, P])
        eps = sb("eps", [P, 1])
        first_root = sb("first_root", [P, 1])
        flags = sb("flags", [P, 6])
        flag_sum = sb("flag_sum", [P, 1])
        far = sb("far", [P, ROUNDS])
        disorder = sb("disorder", [P, 1], I32)

        w_prop = [sb("w_prop1_sb", [P, K, D]), sb("w_prop2_sb", [P, K, D])]
        w_rel = sb("w_rel_sb", [P, REL, K, D])
        b_rel_c = sb("b_rel_c", [P, REL * K])
        b_rel_r = sb("b_rel_r", [1, REL * D])
        w_ih = sb("w_ih_sb", [P, K, 4 * D])
        b_ih = sb("b_ih_sb", [P, 4 * K])
        b_hh = sb("b_hh_sb", [P, 4 * K])
        b_gate = sb("b_gate", [P, 4 * K])
        w1 = sb("w1_sb", [P, K, HALF])
        b1 = sb("b1_sb", [HALF, 1])
        w2 = sb("w2_sb", [HALF, HALF])
        b2 = sb("b2_sb", [HALF, 1])
        w3 = sb("w3_sb", [HALF, D])
        b3 = sb("b3_sb", [1, D])

        def two(name, shape):
            return [sb(f"{name}{v}", shape) for v in range(2)]

        def two_turned(name, shape):
            return [sb(f"{name}{v}", [*shape, n]) for v, n in enumerate((P, LAST_ROWS))]

        sums = sb("sums", [P, K, P])
        out_rows = two("out_rows", [P, REL, D])
        bn = sb("bn", [P, CHUNKS, 6])
        mean_var = sb("mean_var", [P, CHUNKS, 2])
        std = sb("std", [P, CHUNKS])
        rstd = sb("rstd", [P, CHUNKS])
        shift = sb("shift", [P, CHUNKS])
        centred = sb("centred", [P, D])
        hidden = two("hidden", [P, D])
        hidden_t = two_turned("hidden_t", [P, K])
        rel1_t = two_turned("rel1_t", [P, REL, K])
        gate_i = two_turned("gate_i", [P, K])
        gate_g = two_turned("gate_g", [P, K])
        gate_o = two_turned("gate_o", [P, K])
        cell = two_turned("cell", [P, K])
        cell_tanh = two_turned("cell_tanh", [P, K])
        lstm_t = two_turned("lstm_t", [P, K])
        mlp1_t = two_turned("mlp1_t", [HALF])
        mlp2_t = two_turned("mlp2_t", [HALF])

        tile_ps = [bank(f"tile_ps{i}") for i in range(max(BANKS))]
        group_ps = tile_ps[BANKS[0]:BANKS[0] + 2]
        iota_ps = bank("iota_ps")
        ps_a, ps_b, ps_c = ([bank(f"ps_{n}"), tile_ps[i]] for i, n in enumerate("abc"))
        iota_cols = iota_ps[:, 0:BLOCK * SPAN].rearrange("p (t n) -> p t n", n=SPAN)
        one_hot = iota_ps[:, BLOCK * SPAN:2 * BLOCK * SPAN].rearrange("p (t n) -> p t n", n=SPAN)

        dst_in, seq_in, edges_in, weights_in = sem("dst_in"), sem("seq_in"), sem("edges_in"), sem("weights_in")
        x_in = [sem(f"x_in{g}") for g in range(GROUPS)]
        iota_made, const_made, zero_made, identity_made = (
            sem("iota_made"), sem("const_made"), sem("zero_made"), sem("identity_made"))
        eps_made = sem("eps_made")
        settled = sem("settled")
        iota_ready, wide_iota_ready, bias_ready = sem("iota_ready"), sem("wide_iota_ready"), sem("bias_ready")
        edge_step, msg_step, msg_ready = sem("edge_step"), sem("msg_step"), sem("msg_ready")
        starts_ready, flags_ready, disorder_summed, path_ready = (
            sem("starts_ready"), sem("flags_ready"), sem("disorder_summed"), sem("path_ready"))
        group_bn, group_stats, group_std, group_rstd, group_shift, group_hidden, group_centred, group_scaled = (
            sem("group_bn"), sem("group_stats"), sem("group_std"), sem("group_rstd"), sem("group_shift"),
            sem("group_hidden"), sem("group_centred"), sem("group_scaled"))
        hidden_stored = [sem(f"hidden_stored{g}") for g in range(GROUPS)]
        table_stored = [sem(f"table_stored{p}") for p in range(PROPS)]
        staged = [sem(f"staged{h}") for h in range(2)]
        gathered = [sem(f"gathered{s}") for s in range(ROUND)]
        hot_ready, sel_ready, product_done, added = (
            sem("hot_ready"), sem("sel_ready"), sem("product_done"), sem("added"))
        wide_staged, wide_gathered, wide_sel, wide_product, wide_added = (
            sem("wide_staged"), sem("wide_gathered"), sem("wide_sel"), sem("wide_product"), sem("wide_added"))
        sums_ready = [sem(f"sums_ready{p}") for p in range(PROPS)]
        acc_cleared, dense_done = sem("acc_cleared"), sem("dense_done")
        seq_ready, steps_ready = sem("seq_ready"), sem("steps_ready")
        split_step, split_ready = sem("split_step"), sem("split_ready")
        operands_ready, built, accumulated, group_applied, group_added, group_cleared = (
            sem("operands_ready"), sem("built"), sem("accumulated"), sem("group_applied"), sem("group_added"),
            sem("group_cleared"))
        rows_ready = sem("rows_ready")
        x2_ready, bn_ready, stats_ready, std_ready, rstd_ready, shift_ready, hidden_ready = (
            sem("x2_ready"), sem("bn_ready"), sem("stats_ready"), sem("std_ready"), sem("rstd_ready"),
            sem("shift_ready"), sem("hidden_ready"))
        turned, turned_copied, rel1_done, rel1_ready, rel2_done = (
            sem("turned"), sem("turned_copied"), sem("rel1_done"), sem("rel1_ready"), sem("rel2_done"))
        gate_done, gates_ready, cell_ready, cell_tanh_ready, lstm_ready = (
            sem("gate_done"), sem("gates_ready"), sem("cell_ready"), sem("cell_tanh_ready"), sem("lstm_ready"))
        mlp1_done, mlp1_ready, mlp2_done, mlp2_ready, mlp3_done, y_ready, y_stored = (
            sem("mlp1_done"), sem("mlp1_ready"), sem("mlp2_done"), sem("mlp2_ready"), sem("mlp3_done"),
            sem("y_ready"), sem("y_stored"))

        WEIGHTS = 14

        def path(eng):
            eng.wait_ge(path_ready, 1)
            return nc.values_load(disorder[0:1, 0:1], engines=[eng.engine], min_val=0, max_val=1 << 20,
                                  skip_runtime_bounds_check_because="a count of flags, never negative")

        def settle(eng):
            eng.sem_inc(settled, 1)

        def chunk_cols(c):
            return acc[:, :, bass.ds(c * P, P)]

        def chunk_nodes(c):
            return nodes[:, bass.ds(c * D, D)]

        def pair(ps):
            return ps[:, 0:K * P].rearrange("p (k n) -> p k n", k=K)

        def rounds_of(p):
            return GATHER_ROUNDS if p == 0 else ROUNDS

        def uses_before(p, extra):
            return (0, GATHER_ROUNDS, GATHER_ROUNDS + ROUNDS + (1 if extra else 0))[p]

        def is_last(c):
            return isinstance(c, int) and c == CHUNKS - 1

        def work(c):
            return (1, LAST_ROWS) if is_last(c) else (0, P)

        def late_bank(n):
            return (ps_a[0], ps_b[0], ps_c[0])[(n - (SUM_CHUNKS - 1)) % 3]

        def sums_of(c, k):
            return acc[:, k, (CHUNKS - 1) * P:N_NODES] if is_last(c) else sums[:, k, :]

        block = ctx.enter_context(nc.Block())

        @block.sync
        def _(sp):
            for g in range(GROUPS):
                sp.dma_start(nodes[:, g * GC * D:(g + 1) * GC * D].rearrange("p (c f) -> p c f", f=D),
                             x.rearrange("(c p) f -> p c f", p=P)[:, g * GC:(g + 1) * GC, :]).then_inc(x_in[g], 16)
                if g == 0:
                    sp.dma_start(dst_i[:, :], dst_t).then_inc(dst_in, 16)
            sp.dma_start(seq_i[:, :], dst_seq).then_inc(seq_in, 16)
            for to, of in ((src_idx, src_t), (weight, weight_t), (rel_i, rel_t)):
                sp.dma_start(to[:, :], of).then_inc(edges_in, 16)
            def stage(p, i, half):
                index = msg_idx if p == 2 else src_idx
                sp.dma_start(idx_stage[:, half * BLOCK:(half + 1) * BLOCK],
                             index[:, bass.ds((2 * i + half) * BLOCK, BLOCK)]).then_inc(staged[half], 16)

            def indices_read(p, rounds, half):
                for s in range(half * BLOCK, (half + 1) * BLOCK):
                    sp.wait_ge(gathered[s], (rounds + uses_before(p, s < TAIL)) * 16)

            sp.wait_ge(edges_in, 48)
            for half in range(2):
                stage(0, 0, half)
            for g in range(GROUPS):
                a, b = g * GC, (g + 1) * GC
                sp.wait_ge(group_hidden, g + 1)
                if SHARES[g]:
                    sp.wait_ge(group_scaled, sum(SHARES[:g + 1]))
                sp.dma_start(table[0].rearrange("(c p) f -> p c f", p=P)[:, a:b, :], hid[:, a:b, :])\
                    .then_inc(hidden_stored[g], 16)
            for g in range(GROUPS):
                sp.wait_ge(hidden_stored[g], 16)
            for to, of in ((w_prop[0], w_prop1), (w_prop[1], w_prop2), (w_rel, w_rel_t), (b_rel_c, b_rel_cols),
                           (b_rel_r, b_rel_row), (w_ih, w_ih_t), (b_ih, b_ih_cols), (b_hh, b_hh_cols),
                           (w1, w_mlp1), (b1, b_mlp1), (w2, w_mlp2), (b2, b_mlp2), (w3, w_mlp3), (b3, b_mlp3)):
                sp.dma_start(to[:], of).then_inc(weights_in, 16)

            disordered = path(sp)
            with sp.If(disordered == 0):
                for p in range(PROPS):
                    if p > 0:
                        for half in range(2):
                            indices_read(p, 0, half)
                            if p == 2 and half == 0:
                                sp.wait_ge(msg_ready, 1)
                            stage(p, 0, half)
                    with sp.Fori(1, rounds_of(p)) as i:
                        for half in range(2):
                            indices_read(p, i, half)
                            stage(p, i, half)
                    if p > 0:
                        indices_read(p, ROUNDS, 0)
                        stage(p, ROUNDS, 0)
            with sp.Else():
                sp.wait_ge(staged[0], 16)
                sp.wait_ge(msg_ready, 1)
                for p in range(PROPS):
                    index = msg_idx if p == 2 else src_idx
                    with sp.Fori(0, TILES) as j:
                        sp.dma_start(idx_stage[:, 0:1], index[:, bass.ds(j, 1)]).then_inc(wide_staged, 16)
                        sp.wait_ge(wide_gathered, (j + (TILES * p + 1)) * 16)
                        settle(sp)
            sp.wait_ge(y_stored, 16 * CHUNKS)

        @block.gpsimd
        def _(pool):
            nc.gpsimd.memset(eps[:, :], EPS).then_inc(eps_made, 1)
            nc.gpsimd.memset(ones[:, :], 1.0).then_inc(const_made, 1)
            nc.gpsimd.iota(window_i[:], pattern=[[0, BLOCK], [1, SPAN]], base=0, channel_multiplier=0)\
                .then_inc(iota_made, 1)
            nc.gpsimd.iota(final_i[:, :], pattern=[[P, ROUNDS]], base=P, channel_multiplier=0)\
                .then_inc(iota_made, 1)
            nc.gpsimd.iota(row_i[:, :], pattern=[[1, CHUNKS * NARROW]], base=0, channel_multiplier=0)\
                .then_inc(iota_made, 1)
            nc.gpsimd.memset(zeros[:], 0.0).then_inc(const_made, 1)
            nc.gpsimd.memset(identity[:, :], 0.0).then_inc(zero_made, 1)
            nc.gpsimd.memset(acc[:], 0.0).then_inc(const_made, 1)
            nc.gpsimd.memset(part[:], 0.0).then_inc(group_cleared, 1)
            pool.wait_ge(zero_made, 1)
            nc.gpsimd.affine_select(out=identity[:, :], in_=identity[:, :], compare_op=ALU.not_equal, fill=1.0,
                                    base=0, pattern=[[-1, P]], channel_multiplier=1).then_inc(identity_made, 1)

            pool.wait_ge(seq_in, 16)
            nc.gpsimd.tensor_copy(seq_f[:, :], seq_i[:, :]).then_inc(seq_ready, 1)
            pool.wait_ge(seq_ready, 1)
            nc.gpsimd.tensor_tensor(steps[:, :], seq_f[:, 1:TILES + 1], seq_f[:, 0:TILES], ALU.subtract)\
                .then_inc(steps_ready, 1)

            def table_complete(p):
                if p == 0:
                    for g in range(GROUPS):
                        pool.wait_ge(hidden_stored[g], 16)
                else:
                    pool.wait_ge(table_stored[p], 16 * CHUNKS)

            def gather(p, s, out_sem):
                pool.indirect_dma_start(rows[:, s, :], None, table[p][:, :],
                                        bass.IndirectOffsetOnAxis(ap=idx_stage[:, s:s + 1], axis=0))\
                    .then_inc(out_sem, 16)

            def round_(p, i, first, tiles):
                for s in range(tiles):
                    if s % BLOCK == 0:
                        half = s // BLOCK
                        pool.wait_ge(staged[half], (i + (uses_before(p, half * BLOCK < TAIL) + 1)) * 16)
                    if s % 4 == 0 and not first:
                        pool.wait_ge(product_done, i * ROUND + (FIRST_TILE[p] - ROUND + min(s + 4, tiles)))
                        settle(pool)
                    gather(p, s, gathered[s])

            disordered = path(pool)
            with pool.If(disordered == 0):
                for p in range(PROPS):
                    table_complete(p)
                    round_(p, 0, True, ROUND)
                    with pool.Fori(1, rounds_of(p)) as i:
                        round_(p, i, False, ROUND)
                    if p > 0:
                        round_(p, ROUNDS, False, TAIL)
            with pool.Else():
                for p in range(PROPS):
                    table_complete(p)
                    with pool.Fori(0, TILES) as j:
                        pool.wait_ge(wide_staged, (j + (TILES * p + 1)) * 16)
                        settle(pool)
                        gather(p, 0, wide_gathered)
                        pool.wait_ge(wide_product, (j + (TILES * p + 1)) * CHUNKS)

        @block.vector
        def _(dve):
            def group_statistics(g):
                dve.wait_ge(x_in[g], 16)
                for c in range(g * GC, (g + 1) * GC):
                    nc.vector.bn_stats(bn[:, c, :], nodes[:, c * D:(c + 1) * D]).then_inc(group_bn, 1)
                dve.wait_ge(group_bn, (g + 1) * GC)
                for c in range(g * GC, (g + 1) * GC):
                    last = nc.vector.bn_aggr(mean_var[:, c, :], bn[:, c, :])
                last.then_inc(group_stats, 1)

            def group_scale(g):
                a, b = g * GC, (g + 1) * GC
                dve.wait_ge(group_std, g + 1)
                nc.vector.reciprocal(rstd[:, a:b], std[:, a:b]).then_inc(group_rstd, 1)
                dve.wait_ge(group_rstd, g + 1)
                nc.vector.scalar_tensor_tensor(out=shift[:, a:b], in0=mean_var[:, a:b, 0], scalar=-1.0,
                                               in1=rstd[:, a:b], op0=ALU.mult, op1=ALU.mult)\
                    .then_inc(group_shift, 1)

            def group_share(g):
                for n in range(SHARES[g]):
                    c = (g + 1) * GC - SHARES[g] + n
                    done = sum(SHARES[:g]) + n
                    if done > 0:
                        dve.wait_ge(group_scaled, done)
                    nc.vector.tensor_scalar(centred[:, :], nodes[:, c * D:(c + 1) * D], mean_var[:, c, 0:1], 0.0,
                                            ALU.subtract, ALU.max).then_inc(group_centred, 1)
                    dve.wait_ge(group_centred, done + 1)
                    nc.vector.tensor_scalar(hid[:, c, :], centred[:, :], rstd[:, c:c + 1],
                                            None, ALU.mult).then_inc(group_scaled, 1)

            group_statistics(0)
            dve.wait_ge(dst_in, 16)
            nc.vector.tensor_copy(dst_f[:, :], dst_i[:, :]).then_inc(edge_step, 1)
            for g in range(1, GROUPS):
                group_statistics(g)
                group_scale(g - 1)
                group_share(g - 1)
            dve.wait_ge(iota_made, 3)
            nc.vector.tensor_copy(final_cols[:, :], final_i[:, :]).then_inc(edge_step, 1)
            group_scale(GROUPS - 1)
            group_share(GROUPS - 1)

            dve.wait_ge(starts_ready, 1)
            nc.vector.tensor_tensor(dst_off[:, :], dst_f[:, :], ps_a[0][:, 0:COLS], ALU.subtract)\
                .then_inc(edge_step, 1)
            dve.wait_ge(edge_step, 2)
            nc.vector.tensor_tensor(far[:, 0:ROUNDS - 1], ps_a[0][:, ROUND + MARGIN:COLS - MARGIN:ROUND],
                                    final_cols[:, 0:ROUNDS - 1], ALU.is_lt).then_inc(edge_step, 1)
            tile = ROUNDS * ROUND + LAST_MARGIN
            nc.vector.tensor_tensor(far[:, ROUNDS - 1:ROUNDS], ps_a[0][:, tile:tile + 1],
                                    final_cols[:, ROUNDS - 1:ROUNDS], ALU.is_lt).then_inc(edge_step, 1)
            starts = ps_a[0][:, GATHERED:COLS].rearrange("p (g n) -> p g n", n=GROUP)
            nc.vector.tensor_copy(group_first[:, :], starts[:, :, 0]).then_inc(split_step, 1)
            dve.wait_ge(split_step, 1)
            nc.vector.tensor_tensor(place_f[:], starts, group_first[:, :].unsqueeze(2)
                                    .to_broadcast([P, BUILD_GROUPS, GROUP]), ALU.subtract).then_inc(split_step, 1)
            limit = float(BUILT_CHUNKS[0] * P - SPAN)
            nc.vector.tensor_scalar(flags[:, 5:6], ps_a[0][:, GATHERED - 1:GATHERED], limit, None, ALU.is_gt)\
                .then_inc(split_step, 1)
            dve.wait_ge(edge_step, 3)
            nc.vector.tensor_reduce(flags[:, 1:2], dst_off[:, 0:TILES], AX_X, ALU.max).then_inc(edge_step, 1)
            nc.vector.tensor_reduce(flags[:, 3:4], dst_off[:, GATHERED:TILES], AX_X, ALU.max).then_inc(split_step, 1)
            dve.wait_ge(split_step, 2)
            nc.vector.tensor_reduce(flags[:, 4:5], place_f[:], XY, ALU.max).then_inc(split_step, 1)
            dve.wait_ge(steps_ready, 1)
            nc.vector.tensor_reduce(flags[:, 2:3], steps[:, :], AX_X, ALU.min).then_inc(edge_step, 1)
            dve.wait_ge(edge_step, 7)
            dve.wait_ge(split_step, 5)
            nc.vector.tensor_scalar(flags[:, 3:4], flags[:, 3:4], float(NARROW - 1), None, ALU.is_gt)\
                .then_inc(split_step, 1)
            nc.vector.tensor_scalar(flags[:, 4:5], flags[:, 4:5], float(P - NARROW), None, ALU.is_gt)\
                .then_inc(split_step, 1)
            nc.vector.tensor_reduce(flags[:, 0:1], far[:, :], AX_X, ALU.add).then_inc(edge_step, 1)
            nc.vector.tensor_scalar(flags[:, 1:2], flags[:, 1:2], float(SPAN - 1), None, ALU.is_gt)\
                .then_inc(edge_step, 1)
            nc.vector.tensor_scalar(flags[:, 2:3], flags[:, 2:3], 0.0, None, ALU.is_lt).then_inc(edge_step, 1)
            dve.wait_ge(edge_step, 10)
            dve.wait_ge(split_step, 7)
            nc.vector.tensor_reduce(flag_sum[:, :], flags[:, :], AX_X, ALU.add).then_inc(flags_ready, 1)
            dve.wait_ge(disorder_summed, 1)
            nc.vector.tensor_copy(disorder[:, :], ps_b[0][:, 0:1]).then_inc(path_ready, 1)

            def split_sources():
                nc.vector.tensor_scalar(lo_i[:, :], src_idx[:, GATHERED:COLS], P - 1, None, ALU.bitwise_and)\
                    .then_inc(split_step, 1)
                nc.vector.tensor_scalar(hi_i[:, :], src_idx[:, GATHERED:COLS], P.bit_length() - 1, None,
                                        ALU.logical_shift_right).then_inc(split_step, 1)
                nc.vector.tensor_copy(place_i[:, :], place_f[:].rearrange("p g n -> p (g n)"))\
                    .then_inc(split_step, 1)
                dve.wait_ge(split_step, 10)
                nc.vector.tensor_copy(lo_f[:, :], lo_i[:, :]).then_inc(split_ready, 1)
                nc.vector.scalar_tensor_tensor(out=key[:, :], in0=hi_i[:, :], scalar=float(NARROW),
                                               in1=dst_off[:, GATHERED:COLS], op0=ALU.mult, op1=ALU.add)\
                    .then_inc(split_ready, 1)
                dve.wait_ge(split_ready, 2)

            def message_arrays():
                nc.vector.tensor_scalar(msg_idx[:, :], rel_i[:, :], 1.0, float(N_NODES), ALU.is_equal, ALU.mult)\
                    .then_inc(msg_step, 1)
                nc.vector.tensor_scalar(known[:, :], rel_i[:, :], 0.0, None, ALU.is_equal).then_inc(msg_step, 1)
                dve.wait_ge(msg_step, 2)
                nc.vector.scalar_tensor_tensor(out=known[:, :], in0=rel_i[:, :], scalar=1.0, in1=known[:, :],
                                               op0=ALU.is_equal, op1=ALU.add).then_inc(msg_step, 1)
                nc.vector.tensor_tensor(msg_idx[:, :], msg_idx[:, :], src_idx[:, :], ALU.add).then_inc(msg_ready, 1)
                dve.wait_ge(msg_step, 3)

            def gate_bias():
                dve.wait_ge(weights_in, 16 * WEIGHTS)
                nc.vector.tensor_tensor(b_gate[:, :], b_ih[:, :], b_hh[:, :], ALU.add).then_inc(bias_ready, 1)

            def build_block(p, b, half):
                value = known if p == 2 else weight
                cols = bass.ds(b * BLOCK, BLOCK)
                if p > 0 or not isinstance(b, int) or b > 0:
                    dve.wait_ge(sel_ready, b + FIRST_BLOCK[p])
                nc.vector.tensor_tensor(one_hot, iota_cols,
                                        dst_off[:, cols].unsqueeze(2).to_broadcast([P, BLOCK, SPAN]),
                                        ALU.is_equal).then_inc(hot_ready, 1)
                dve.wait_ge(hot_ready, b + (FIRST_BLOCK[p] + 1))
                nc.vector.tensor_tensor(sel[:, half * BLOCK:(half + 1) * BLOCK, :], one_hot,
                                        value[:, cols].unsqueeze(2).to_broadcast([P, BLOCK, SPAN]),
                                        ALU.mult).then_inc(sel_ready, 1)

            def first_destinations(b):
                _, starts = nc.values_load_multi_w_load_instructions(
                    dst_i[0:1, bass.ds(b * BLOCK, BLOCK)], engines=[dve.engine], min_val=0,
                    max_val=N_NODES - 1, skip_runtime_bounds_check_because="destinations are nodes")
                return starts

            def add_tile(p, i, s, start):
                dve.wait_ge(product_done, i * ROUND + (FIRST_TILE[p] + s + 1))
                if p > 0 or s > 0 or not isinstance(i, int) or i > 0:
                    dve.wait_ge(added, i * ROUND + (FIRST_TILE[p] + s))
                window = acc[:, :, bass.ds(start, SPAN)]
                own = (s % SIDE) * SPAN
                nc.vector.tensor_tensor(window, pair(tile_ps[s % BANKS[p]])[:, :, own:own + SPAN], window, ALU.add)\
                    .then_inc(added, 1)

            def residual(c):
                v, n = work(c)
                x_rows = chunk_nodes(c)[0:n, :]
                dve.wait_ge(dense_done, c + (CHUNKS + 1))
                nc.vector.tensor_tensor(x_rows, ps_a[v][0:n, 0:D], x_rows, ALU.add).then_inc(x2_ready, 1)
                dve.wait_ge(x2_ready, c + 1)
                settle(dve)
                nc.vector.bn_stats(bn[0:n, v, :], x_rows).then_inc(bn_ready, 1)
                dve.wait_ge(bn_ready, c + 1)
                settle(dve)
                nc.vector.bn_aggr(mean_var[0:n, v, :], bn[0:n, v, :]).then_inc(stats_ready, 1)

            def norm_scale(c):
                v, n = work(c)
                dve.wait_ge(std_ready, c + 1)
                nc.vector.reciprocal(rstd[0:n, v:v + 1], std[0:n, v:v + 1]).then_inc(rstd_ready, 1)
                dve.wait_ge(rstd_ready, c + 1)
                nc.vector.scalar_tensor_tensor(out=shift[0:n, v:v + 1], in0=mean_var[0:n, v, 0:1], scalar=-1.0,
                                               in1=rstd[0:n, v:v + 1], op0=ALU.mult, op1=ALU.mult)\
                    .then_inc(shift_ready, 1)

            iota_f = hid[:].rearrange("p c f -> p (c f)")

            def cell_state(c):
                v, n = work(c)
                dve.wait_ge(gates_ready, c + 1)
                nc.vector.tensor_tensor(cell[v][:, :, 0:n], gate_i[v][:, :, 0:n], gate_g[v][:, :, 0:n], ALU.mult)\
                    .then_inc(cell_ready, 1)

            def lstm_out(c):
                v, n = work(c)
                dve.wait_ge(cell_tanh_ready, c + 1)
                nc.vector.tensor_tensor(lstm_t[v][:, :, 0:n], gate_o[v][:, :, 0:n], cell_tanh[v][:, :, 0:n],
                                        ALU.mult).then_inc(lstm_ready, 1)

            def result(c):
                v, n = work(c)
                dve.wait_ge(mlp3_done, c + 1)
                if v == 0 and not (isinstance(c, int) and c == 0):
                    dve.wait_ge(y_stored, c * 16)
                nc.vector.tensor_tensor(out_rows[v][0:n, 0, :], ps_c[v][0:n, 0:D],
                                        chunk_nodes(c)[0:n, :], ALU.add).then_inc(y_ready, 1)

            def chunk_step(p, c, s):
                if p == 1:
                    if s == 9:
                        residual(c)
                    if s == 10:
                        norm_scale(c)
                if p == 2:
                    if s == 13:
                        cell_state(c)
                    if s == 14:
                        lstm_out(c)
                    if s == 2:
                        result(c)

            def whole_chunk(p, c):
                for s in (*range(BLOCK, ROUND), *range(BLOCK)):
                    chunk_step(p, c, s)

            def last_chunks(p):
                a, b = CHUNKS - 2, CHUNKS - 1
                if p == 1:
                    residual(a)
                    norm_scale(a)
                    residual(b)
                    norm_scale(b)
                if p == 2:
                    cell_state(a)
                    lstm_out(a)
                    cell_state(b)
                    lstm_out(b)
                    result(a)
                    result(b)

            def operands(u, n):
                j = u * GROUP + n
                nc.vector.tensor_scalar(weighted_lo[:, n % AHEAD, :], row_f[:, 0:P], lo_f[:, bass.ds(j, 1)],
                                        weight[:, bass.ds(j + GATHERED, 1)], ALU.is_equal, ALU.mult)\
                    .then_inc(operands_ready, 1)
                nc.vector.tensor_scalar(keyed[:, n % AHEAD, :, :].rearrange("p c n -> p (c n)"), row_f[:, :],
                                        key[:, bass.ds(j, 1)], None, ALU.is_equal).then_inc(operands_ready, 1)

            def accumulate(u, n, place):
                dve.wait_ge(built, u * GROUP + (n + 1))
                if n == 0:
                    dve.wait_ge(group_cleared, u + 1)
                else:
                    dve.wait_ge(accumulated, u * GROUP + n)
                window = part[:, :, bass.ds(place, NARROW)]
                nc.vector.tensor_tensor(window, group_ps[n % 2][:, 0:CHUNKS * NARROW]
                                        .rearrange("p (c n) -> p c n", n=NARROW), window, ALU.add)\
                    .then_inc(accumulated, 1)

            def places(u, n):
                _, found = nc.values_load_multi_w_load_instructions(
                    place_i[0:1, bass.ds(u * GROUP + n, GROUP // 2)], engines=[dve.engine], min_val=0,
                    max_val=P - NARROW, skip_runtime_bounds_check_because="the choice of the path rests on it")
                return found

            def group_add(u):
                _, first = nc.values_load_multi_w_load_instructions(
                    dst_i[0:1, bass.ds(u * GROUP + GATHERED, 1)], engines=[dve.engine], min_val=0,
                    max_val=N_NODES - 1, skip_runtime_bounds_check_because="destinations are nodes")
                dve.wait_ge(group_applied, u + 1)
                dve.wait_ge(added, (u * GROUP_ROUNDS + 1) * ROUND + (GROUP_ADD_STEP + 1))
                window = acc[:, :, bass.ds(first[0], P)]
                nc.vector.tensor_tensor(window, pair(group_ps[0]), window, ALU.add).then_inc(group_added, 1)
                dve.wait_ge(group_added, u + 2)

            def build_steps(u, q, starts_of):
                if q < AHEAD - 1:
                    operands(u, q)
                if q == AHEAD - 1:
                    starts_of[:] = places(u, 0)
                    operands(u, q)
                if q in BUILD_STEPS and q > BUILD_STEPS[0]:
                    n = BUILD_STEPS.index(q)
                    if n - 1 == GROUP // 2:
                        starts_of[:] = places(u, GROUP // 2)
                    accumulate(u, n - 1, starts_of[(n - 1) % (GROUP // 2)])
                    if n + AHEAD - 1 < GROUP:
                        operands(u, n + AHEAD - 1)
                if q == APPLY_STEP - 1:
                    accumulate(u, GROUP - 1, starts_of[GROUP // 2 - 1])
                if q == GROUP_ADD_STEP:
                    group_add(u)

            def round_(p, i, late, early, tiles, group=None, group_round=0, places_now=None):
                for s in range(tiles):
                    if s % BLOCK == 0:
                        starts = first_destinations(2 * i + s // BLOCK)
                    add_tile(p, i, s, starts[s % BLOCK])
                    if s == BUILD_AT and tiles == ROUND:
                        build_block(p, 2 * i + 1, 1)
                    if s == BLOCK + BUILD_AT and not (p == 0 and isinstance(i, int) and i == GATHER_ROUNDS - 1):
                        build_block(p, 2 * i + 2, 0)
                    chunk = late if s < BLOCK else early
                    if chunk is not None:
                        chunk_step(p, chunk, s)
                    if group is not None:
                        build_steps(group, group_round * ROUND + s, places_now)

            nc.vector.tensor_copy(iota_cols, window_i[:]).then_inc(iota_ready, 1)
            nc.vector.tensor_copy(row_f[:, :], row_i[:, :]).then_inc(iota_ready, 1)
            dve.wait_ge(edges_in, 48)
            dve.wait_ge(iota_ready, 2)
            dve.wait_ge(const_made, 3)
            disordered = path(dve)
            with dve.If(disordered == 0):
                build_block(0, 0, 0)
                round_(0, 0, None, None, ROUND)
                split_sources()
                dve.sem_inc(group_added, 1)
                with dve.Fori(0, BUILD_GROUPS) as u:
                    places_now = []
                    for q in range(GROUP_ROUNDS):
                        round_(0, u * GROUP_ROUNDS + (q + 1), None, None, ROUND, u, q, places_now)
                round_(0, GATHER_ROUNDS - 1, None, None, ROUND)
                message_arrays()
                for p in range(1, PROPS):
                    dve.wait_ge(acc_cleared, CHUNKS * p)
                    build_block(p, 0, 0)
                    round_(p, 0, None, None, ROUND)
                    if p == 1:
                        gate_bias()
                    round_(p, 1, None, 0, ROUND)
                    with dve.Fori(2, ROUNDS) as i:
                        round_(p, i, i - 2, i - 1, ROUND)
                    round_(p, ROUNDS, ROUNDS - 2, None, TAIL)
                    last_chunks(p)
            with dve.Else():
                message_arrays()
                gate_bias()
                for g in range(GROUPS):
                    dve.wait_ge(hidden_stored[g], 16)
                for w in range(CHUNKS):
                    nc.vector.tensor_scalar(hid[:, w, 0:P], row_f[:, 0:P], float(w * P), None, ALU.add)\
                        .then_inc(wide_iota_ready, 1)
                dve.wait_ge(wide_iota_ready, CHUNKS)
                for p in range(PROPS):
                    value = known if p == 2 else weight
                    if p > 0:
                        dve.wait_ge(acc_cleared, CHUNKS * p)
                    with dve.Fori(0, TILES) as j:
                        with dve.Fori(0, CHUNKS) as w:
                            done = (j + TILES * p) * CHUNKS + w + 1
                            nc.vector.tensor_scalar(sel_wide[:, :], iota_f[:, bass.ds(w * D, P)],
                                                    dst_f[:, bass.ds(j, 1)], value[:, bass.ds(j, 1)],
                                                    ALU.is_equal, ALU.mult).then_inc(wide_sel, 1)
                            dve.wait_ge(wide_product, done)
                            nc.vector.tensor_tensor(chunk_cols(w), pair(tile_ps[0]), chunk_cols(w), ALU.add)\
                                .then_inc(wide_added, 1)
                            dve.wait_ge(wide_added, done)
                    if p > 0:
                        whole_chunk(p, 0)
                        with dve.Fori(1, CHUNKS - 1) as c:
                            whole_chunk(p, c)
                        whole_chunk(p, CHUNKS - 1)

        @block.scalar
        def _(act):
            act.wait_ge(eps_made, 1)
            nc.scalar.activation(first_root[:, :], eps[:, :], ACT.Sqrt).then_inc(settled, 1)
            def group_deviation(g):
                a, b = g * GC, (g + 1) * GC
                act.wait_ge(group_stats, g + 1)
                nc.scalar.activation(std[:, a:b], mean_var[:, a:b, 1], ACT.Sqrt, bias=eps[:, 0:1])\
                    .then_inc(group_std, 1)

            group_deviation(0)
            for g in range(GROUPS):
                a, b = g * GC, (g + 1) * GC
                if g < GROUPS - 1:
                    group_deviation(g + 1)
                act.wait_ge(group_shift, g + 1)
                for c in range(a, b - SHARES[g]):
                    last = nc.scalar.activation(hid[:, c, :], nodes[:, c * D:(c + 1) * D], ACT.Relu,
                                                bias=shift[:, c:c + 1], scale=rstd[:, c:c + 1])
                last.then_inc(group_hidden, 1)
            act.wait_ge(const_made, 3)

            def take_sums(p, c):
                nc.scalar.activation(sums[:], chunk_cols(c), ACT.Copy).then_inc(sums_ready[p], 1)
                if p < PROPS - 1:
                    act.wait_ge(sums_ready[p], c + 1)
                    settle(act)
                    nc.scalar.activation(chunk_cols(c), zeros[:], ACT.Copy).then_inc(acc_cleared, 1)

            def clear_last(p):
                if p < PROPS - 1:
                    act.wait_ge(dense_done, CHUNKS * (p + 1))
                    nc.scalar.activation(chunk_cols(CHUNKS - 1), zeros[:], ACT.Copy).then_inc(acc_cleared, 1)

            def buffer_free(p, c):
                if not is_last(c) and not (isinstance(c, int) and c == 0):
                    act.wait_ge(table_stored[p], c * 16)
                    settle(act)

            def mid_rows(c, shared=True):
                v, n = work(c)
                y = out_rows[v][0:n, 0, :]
                if shared:
                    buffer_free(1, c)
                act.wait_ge(dense_done, c + 1)
                settle(act)
                nc.scalar.activation(y, ps_a[v][0:n, 0:D], ACT.Copy).then_inc(rows_ready, 1)
                act.wait_ge(rows_ready, c + 1)
                act.dma_start(table[1][bass.ds(c * P, n), :], y).then_inc(table_stored[1], 16)

            def deviation(c):
                v, n = work(c)
                act.wait_ge(stats_ready, c + 1)
                nc.scalar.activation(std[0:n, v:v + 1], mean_var[0:n, v, 1:2], ACT.Sqrt, bias=eps[0:n, 0:1])\
                    .then_inc(std_ready, 1)

            def norm(c):
                v, n = work(c)
                act.wait_ge(shift_ready, c + 1)
                settle(act)
                nc.scalar.activation(hidden[v][0:n, :], chunk_nodes(c)[0:n, :], ACT.Relu, bias=shift[0:n, v:v + 1],
                                     scale=rstd[0:n, v:v + 1]).then_inc(hidden_ready, 1)

            def copy_turned(c):
                v, n = work(c)
                act.wait_ge(turned, c + 1)
                nc.scalar.activation(hidden_t[v][:, :, 0:n], pair(ps_b[v])[:, :, 0:n], ACT.Copy)\
                    .then_inc(turned_copied, 1)

            def rel_first(c):
                v, n = work(c)
                for r, ps in enumerate((ps_c[v], ps_b[v])):
                    act.wait_ge(rel1_done, REL * c + (r + 1))
                    for m in range(K):
                        q = r * K + m
                        done = nc.scalar.activation(rel1_t[v][:, r, m, 0:n], ps[:, m * P:m * P + n], ACT.Relu,
                                                    bias=b_rel_c[:, q:q + 1])
                    done.then_inc(rel1_ready, 1)

            def message_rows(c):
                v, n = work(c)
                buffer_free(2, c)
                for r, ps in enumerate((ps_a[v], ps_c[v])):
                    act.wait_ge(rel2_done, REL * c + (r + 1))
                    settle(act)
                    nc.scalar.activation(out_rows[v][0:n, r, :], ps[0:n, 0:D], ACT.Relu)\
                        .then_inc(rows_ready, 1)
                act.wait_ge(rows_ready, REL * c + (CHUNKS + REL))
                act.dma_start(table[2].rearrange("(r n) f -> n r f", r=REL)[bass.ds(c * P, n), :, :],
                              out_rows[v][0:n, :, :]).then_inc(table_stored[2], 16)

            def gates(c):
                v, n = work(c)
                for t, (ps, to, gate, func) in enumerate((
                        (ps_a, gate_i, 0, ACT.Sigmoid), (ps_b, gate_g, 2, ACT.Tanh),
                        (ps_c, gate_o, 3, ACT.Sigmoid))):
                    act.wait_ge(gate_done, GATES * c + (t + 1))
                    for m in range(K):
                        done = nc.scalar.activation(to[v][:, m, 0:n], ps[v][:, m * P:m * P + n], func,
                                                    bias=b_gate[:, gate * K + m:gate * K + m + 1])
                done.then_inc(gates_ready, 1)

            def tanh_cell(c):
                v, n = work(c)
                act.wait_ge(cell_ready, c + 1)
                nc.scalar.activation(cell_tanh[v][:, :, 0:n], cell[v][:, :, 0:n], ACT.Tanh)\
                    .then_inc(cell_tanh_ready, 1)

            def mlp_first(c):
                v, n = work(c)
                act.wait_ge(mlp1_done, c + 1)
                nc.scalar.activation(mlp1_t[v][:, 0:n], ps_a[v][:, 0:n], ACT.Relu, bias=b1[:, 0:1])\
                    .then_inc(mlp1_ready, 1)

            def mlp_second(c):
                v, n = work(c)
                act.wait_ge(mlp2_done, c + 1)
                nc.scalar.activation(mlp2_t[v][:, 0:n], ps_a[v][:, P:P + n], ACT.Relu, bias=b2[:, 0:1])\
                    .then_inc(mlp2_ready, 1)

            def store_result(c):
                v, n = work(c)
                act.wait_ge(y_ready, c + 1)
                act.dma_start(out[bass.ds(c * P, n), :], out_rows[v][0:n, 0, :]).then_inc(y_stored, 16)

            def chunk(p, c):
                if is_last(c):
                    clear_last(p)
                else:
                    take_sums(p, c)
                if p == 0:
                    mid_rows(c)
                if p == 1:
                    deviation(c)
                    norm(c)
                    copy_turned(c)
                    rel_first(c)
                    message_rows(c)
                if p == 2:
                    gates(c)
                    tanh_cell(c)
                    mlp_first(c)
                    mlp_second(c)
                    store_result(c)

            def last_chunks(p):
                a, b = CHUNKS - 2, CHUNKS - 1
                take_sums(p, a)
                if p == 1:
                    deviation(a)
                    norm(a)
                    deviation(b)
                    copy_turned(a)
                    norm(b)
                    clear_last(p)
                    rel_first(a)
                    copy_turned(b)
                    message_rows(a)
                    rel_first(b)
                    message_rows(b)
                if p == 2:
                    gates(a)
                    tanh_cell(a)
                    gates(b)
                    mlp_first(a)
                    tanh_cell(b)
                    mlp_second(a)
                    mlp_first(b)
                    mlp_second(b)
                    store_result(a)
                    store_result(b)

            def late_mid_rows(n, c):
                rows_n = LAST_ROWS if is_last(c) else P
                act.wait_ge(dense_done, n + 1)
                nc.scalar.activation(hid[0:rows_n, c, :], late_bank(n)[0:rows_n, 0:D], ACT.Copy)\
                    .then_inc(rows_ready, 1)
                act.wait_ge(rows_ready, n + 1)
                act.dma_start(table[1][c * P:c * P + rows_n, :], hid[0:rows_n, c, :]).then_inc(table_stored[1], 16)

            disordered = path(act)
            act.wait_ge(weights_in, 16 * WEIGHTS)
            with act.If(disordered == 0):
                with act.Fori(0, BUILD_GROUPS) as u:
                    for q in range(GROUP_ROUNDS):
                        act.wait_ge(added, (u * GROUP_ROUNDS + q) * ROUND + (ROUND + MARGIN))
                        settle(act)
                        c = u * GROUP_ROUNDS + q
                        take_sums(0, c)
                        mid_rows(c, False)
                        act.wait_ge(table_stored[1], (c + 1) * 16)
                    act.wait_ge(group_added, u + 2)
                    settle(act)
                    nc.scalar.activation(part[:], zeros[:, 0:1, :].to_broadcast([P, CHUNKS, P]), ACT.Copy)\
                        .then_inc(group_cleared, 1)
                for n, c in enumerate(LATE_CHUNKS, SUM_CHUNKS):
                    late_mid_rows(n, c)
                for c in LATE_CHUNKS:
                    nc.scalar.activation(chunk_cols(c), zeros[:], ACT.Copy).then_inc(acc_cleared, 1)
                for p in range(1, PROPS):
                    if p == 2:
                        act.wait_ge(bias_ready, 1)
                    act.wait_ge(added, FIRST_TILE[p] + ROUND + MARGIN)
                    chunk(p, 0)
                    with act.Fori(1, ROUNDS - 1) as c:
                        act.wait_ge(added, c * ROUND + (FIRST_TILE[p] + ROUND + MARGIN))
                        settle(act)
                        chunk(p, c)
                    act.wait_ge(added, FIRST_TILE[p] + ROUNDS * ROUND + LAST_MARGIN)
                    last_chunks(p)
            with act.Else():
                for p in range(PROPS):
                    if p == 2:
                        act.wait_ge(bias_ready, 1)
                    act.wait_ge(wide_added, TILES * CHUNKS * (p + 1))
                    chunk(p, 0)
                    with act.Fori(1, CHUNKS - 1) as c:
                        chunk(p, c)
                    chunk(p, CHUNKS - 1)

        @block.tensor
        def _(pe):
            pe.wait_ge(const_made, 1)
            pe.wait_ge(edge_step, 1)
            nc.tensor.matmul(ps_a[0][:, 0:COLS], ones[0:1, :], dst_f[0:1, :], start=True, stop=True)\
                .then_inc(starts_ready, 1)
            pe.wait_ge(flags_ready, 1)
            nc.tensor.matmul(ps_b[0][:, 0:1], ones[:, :], flag_sum[:, :], start=True, stop=True)\
                .then_inc(disorder_summed, 1)
            pe.wait_ge(identity_made, 1)

            def tile(p, i, s):
                j = i * ROUND + (FIRST_TILE[p] + s)
                if s % BLOCK == 0:
                    pe.wait_ge(sel_ready, 2 * i + (FIRST_BLOCK[p] + s // BLOCK + 1))
                pe.wait_ge(gathered[s], (i + (uses_before(p, s < TAIL) + 1)) * 16)
                if p > 0 or s >= BANKS[p] or not isinstance(i, int) or i > 0:
                    pe.wait_ge(added, j - (BANKS[p] - 1))
                side = s - s % SIDE
                for k in range(K):
                    last = nc.tensor.matmul(tile_ps[s % BANKS[p]][:, k * P:(k + 1) * P], rows[:, s, k * P:(k + 1) * P],
                                            sel[:, side:side + SIDE, :], start=True, stop=True)
                last.then_inc(product_done, 1)

            def wait_for_sums(c, p):
                if not is_last(c):
                    pe.wait_ge(sums_ready[p], c + 1)

            def apply(c, p):
                v, n = work(c)
                wait_for_sums(c, p)
                for k in range(K):
                    last = nc.tensor.matmul(ps_a[v][0:n, 0:D], sums_of(c, k), w_prop[p][:, k, :], start=(k == 0),
                                            stop=(k == K - 1))
                last.then_inc(dense_done, 1)

            def turn(c):
                v, n = work(c)
                pe.wait_ge(hidden_ready, c + 1)
                for k in range(K):
                    last = nc.tensor.transpose(ps_b[v][:, k * P:k * P + n], hidden[v][0:n, k * P:(k + 1) * P],
                                               identity[0:n, 0:n])
                last.then_inc(turned, 1)

            def rel_first(c, r):
                v, n = work(c)
                ps = (ps_c[v], ps_b[v])[r]
                if r == 0:
                    pe.wait_ge(turned_copied, c + 1)
                for m in range(K):
                    for k in range(K):
                        last = nc.tensor.matmul(ps[:, m * P:m * P + n], w_rel[:, r, k, m * P:(m + 1) * P],
                                                hidden_t[v][:, k, 0:n], start=(k == 0), stop=(k == K - 1))
                last.then_inc(rel1_done, 1)

            def rel_second(c, r):
                v, n = work(c)
                cols = (ps_a[v], ps_c[v])[r][0:n, 0:D]
                nc.tensor.matmul(cols, ones[0:1, 0:n], b_rel_r[0:1, r * D:(r + 1) * D], start=True, stop=False)
                pe.wait_ge(rel1_ready, REL * c + (r + 1))
                for k in range(K):
                    last = nc.tensor.matmul(cols, rel1_t[v][:, r, k, 0:n], w_rel[:, r, k, :], start=False,
                                            stop=(k == K - 1))
                last.then_inc(rel2_done, 1)

            def gate_product(c, t):
                v, n = work(c)
                ps, gate = ((ps_a[v], 0), (ps_b[v], 2), (ps_c[v], 3))[t]
                if t == 0:
                    wait_for_sums(c, 2)
                for m in range(K):
                    col = gate * D + m * P
                    for k in range(K):
                        last = nc.tensor.matmul(ps[:, m * P:m * P + n], w_ih[:, k, col:col + P],
                                                sums_of(c, k), start=(k == 0), stop=(k == K - 1))
                last.then_inc(gate_done, 1)

            def mlp_first(c):
                v, n = work(c)
                pe.wait_ge(lstm_ready, c + 1)
                for k in range(K):
                    last = nc.tensor.matmul(ps_a[v][:, 0:n], w1[:, k, :], lstm_t[v][:, k, 0:n], start=(k == 0),
                                            stop=(k == K - 1))
                last.then_inc(mlp1_done, 1)

            def mlp_second(c):
                v, n = work(c)
                pe.wait_ge(mlp1_ready, c + 1)
                nc.tensor.matmul(ps_a[v][:, P:P + n], w2[:, :], mlp1_t[v][:, 0:n], start=True, stop=True)\
                    .then_inc(mlp2_done, 1)

            def mlp_third(c):
                v, n = work(c)
                cols = ps_c[v][0:n, 0:D]
                nc.tensor.matmul(cols, ones[0:1, 0:n], b3[0:1, :], start=True, stop=False)
                pe.wait_ge(mlp2_ready, c + 1)
                nc.tensor.matmul(cols, mlp2_t[v][:, 0:n], w3[:, :], start=False, stop=True).then_inc(mlp3_done, 1)

            def chunk_step(p, c, s):
                if p < 2 and s == 8:
                    apply(c, p)
                if p == 1:
                    if s == 13:
                        turn(c)
                    if s == 15:
                        rel_first(c, 0)
                    if s == 0:
                        rel_first(c, 1)
                    if s == 1:
                        rel_second(c, 0)
                    if s == 2:
                        rel_second(c, 1)
                if p == 2:
                    if s == 8:
                        gate_product(c, 0)
                    if s == 10:
                        gate_product(c, 1)
                    if s == 12:
                        gate_product(c, 2)
                    if s == 15:
                        mlp_first(c)
                    if s == 0:
                        mlp_second(c)
                    if s == 1:
                        mlp_third(c)

            def whole_chunk(p, c):
                for s in (*range(BLOCK, ROUND), *range(BLOCK)):
                    chunk_step(p, c, s)

            def tail_step(p, s):
                a = CHUNKS - 2
                if p == 2 and s in (4, 5, 6):
                    gate_product(a, s - 4)

            def keep_busy(n):
                for _ in range(n):
                    nc.tensor.matmul(tile_ps[-1][:, 0:D], identity[:, :], zeros[:].rearrange("p k n -> p (k n)"),
                                     start=True, stop=True)

            def last_chunks(p):
                a, b = CHUNKS - 2, CHUNKS - 1
                if p == 1:
                    apply(a, p)
                pe.wait_ge(added, FIRST_TILE[p] + TILES)
                if p == 1:
                    apply(b, p)
                    keep_busy(5)
                    turn(a)
                    rel_first(a, 0)
                    rel_first(a, 1)
                    turn(b)
                    rel_second(a, 0)
                    rel_second(a, 1)
                    rel_first(b, 0)
                    rel_first(b, 1)
                    rel_second(b, 0)
                    rel_second(b, 1)
                if p == 2:
                    gate_product(b, 0)
                    gate_product(b, 1)
                    gate_product(b, 2)
                    mlp_first(a)
                    mlp_second(a)
                    keep_busy(1)
                    mlp_third(a)
                    keep_busy(1)
                    mlp_first(b)
                    mlp_second(b)
                    mlp_third(b)

            def build(u, n):
                pe.wait_ge(operands_ready, (u * GROUP + n) * 2 + 2)
                if n == 0:
                    pe.wait_ge(group_added, u + 1)
                if n >= 2:
                    pe.wait_ge(accumulated, u * GROUP + (n - 1))
                nc.tensor.matmul(group_ps[n % 2][:, 0:CHUNKS * NARROW], weighted_lo[:, n % AHEAD, :],
                                 keyed[:, n % AHEAD, :, :], start=True, stop=True).then_inc(built, 1)

            def build_steps(u, q):
                if q in BUILD_STEPS:
                    build(u, BUILD_STEPS.index(q))
                if q == APPLY_STEP:
                    pe.wait_ge(accumulated, (u + 1) * GROUP)
                for m in range((q - APPLY_STEP) * APPLY_WIDTH, (q - APPLY_STEP + 1) * APPLY_WIDTH):
                    if 0 <= m < K * CHUNKS:
                        k, c = m // CHUNKS, m % CHUNKS
                        last = nc.tensor.matmul(group_ps[0][:, k * P:(k + 1) * P], hid[:, c, k * P:(k + 1) * P],
                                                part[:, c, :], start=(c == 0), stop=(c == CHUNKS - 1))
                        if m == K * CHUNKS - 1:
                            last.then_inc(group_applied, 1)

            def late_apply(n, c):
                rows_n = LAST_ROWS if is_last(c) else P
                pe.wait_ge(rows_ready, n - 2)
                for k in range(K):
                    last = nc.tensor.matmul(late_bank(n)[0:rows_n, 0:D], acc[:, k, c * P:c * P + rows_n],
                                            w_prop[0][:, k, :], start=(k == 0), stop=(k == K - 1))
                last.then_inc(dense_done, 1)

            def first_round_(i, u, q):
                for s in range(ROUND):
                    tile(0, i, s)
                    if s == BLOCK:
                        apply(i - 1, 0)
                    build_steps(u, q * ROUND + s)

            def round_(p, i, late, early, tiles):
                for s in range(tiles):
                    tile(p, i, s)
                    chunk = late if s < BLOCK else early
                    if chunk is not None:
                        chunk_step(p, chunk, s)
                    if tiles == TAIL:
                        tail_step(p, s)

            disordered = path(pe)
            with pe.If(disordered == 0):
                round_(0, 0, None, None, ROUND)
                pe.wait_ge(weights_in, 16 * WEIGHTS)
                pe.wait_ge(group_hidden, GROUPS)
                pe.wait_ge(group_scaled, sum(SHARES))
                with pe.Fori(0, BUILD_GROUPS) as u:
                    for q in range(GROUP_ROUNDS):
                        first_round_(u * GROUP_ROUNDS + (q + 1), u, q)
                pe.wait_ge(group_added, BUILD_GROUPS + 1)
                for s in range(ROUND):
                    tile(0, GATHER_ROUNDS - 1, s)
                    if s in LATE_STEPS:
                        n = LATE_STEPS[s]
                        if n == len(BUILT_CHUNKS):
                            pe.wait_ge(added, (GATHER_ROUNDS - 1) * ROUND + MARGIN)
                        late_apply(SUM_CHUNKS + n, LATE_CHUNKS[n])
                pe.wait_ge(added, GATHERED)
                for n in range(len(LATE_STEPS), len(LATE_CHUNKS)):
                    late_apply(SUM_CHUNKS + n, LATE_CHUNKS[n])
                for p in range(1, PROPS):
                    round_(p, 0, None, None, ROUND)
                    round_(p, 1, None, 0, ROUND)
                    with pe.Fori(2, ROUNDS) as i:
                        round_(p, i, i - 2, i - 1, ROUND)
                    round_(p, ROUNDS, ROUNDS - 2, None, TAIL)
                    last_chunks(p)
            with pe.Else():
                pe.wait_ge(weights_in, 16 * WEIGHTS)
                for p in range(PROPS):
                    with pe.Fori(0, TILES) as j:
                        pe.wait_ge(wide_gathered, (j + (TILES * p + 1)) * 16)
                        settle(pe)
                        with pe.Fori(0, CHUNKS) as w:
                            pe.wait_ge(wide_sel, (j + TILES * p) * CHUNKS + w + 1)
                            for k in range(K):
                                last = nc.tensor.matmul(tile_ps[0][:, k * P:(k + 1) * P],
                                                        rows[:, 0, k * P:(k + 1) * P], sel_wide[:, :],
                                                        start=True, stop=True)
                            last.then_inc(wide_product, 1)
                    with pe.Fori(0, CHUNKS - 1) as c:
                        whole_chunk(p, c)
                    pe.wait_ge(wide_added, TILES * CHUNKS * (p + 1))
                    whole_chunk(p, CHUNKS - 1)


def kernel(x, src, dst, edge_type_2, edge_weight, L0_gnn_W1, L0_gnn_W2, L1_gnn_W_rel, L1_gnn_b_rel, L1_gnn_W_ih,
           L1_gnn_b_ih, L1_gnn_b_hh, L1_gnn_W1, L1_gnn_b1, L1_gnn_W2, L1_gnn_b2, L1_gnn_W3, L1_gnn_b3):
    import concourse.bacc as bacc
    from concourse.bass_utils import run_bass_kernel_spmd

    def tiled(a, fill):
        a = np.asarray(a)
        return np.ascontiguousarray(
            np.concatenate([a, np.full(COLS * P - N_EDGES, fill, a.dtype)]).reshape(COLS, P).T)

    def halves(a):
        return np.ascontiguousarray(a.reshape(K, P, a.shape[1]).transpose(1, 0, 2))

    def cols(a):
        return np.ascontiguousarray(np.asarray(a).reshape(-1, P).T)

    x = np.asarray(x)
    dst = np.asarray(dst)
    w_rel = np.asarray(L1_gnn_W_rel)
    in_order = np.concatenate([dst, np.full(TILES * (P + 1) - N_EDGES, N_NODES - 1, dst.dtype)])
    arrays = {
        "x": np.concatenate([x, np.zeros((NODES - N_NODES, D), x.dtype)]),
        "src_t": tiled(src, 0),
        "dst_t": tiled(dst, N_NODES - 1),
        "dst_seq": np.ascontiguousarray(np.concatenate(
            [in_order[:P * TILES].reshape(P, TILES), in_order[TILES:].reshape(P, TILES)[:, 0:1]], axis=1)),
        "rel_t": tiled(edge_type_2, PAD_REL),
        "weight_t": tiled(edge_weight, 0),
        "w_prop1": halves(np.asarray(L0_gnn_W1)),
        "w_prop2": halves(np.asarray(L0_gnn_W2)),
        "w_rel_t": np.ascontiguousarray(w_rel.transpose(0, 2, 1).reshape(REL, K, P, D).transpose(2, 0, 1, 3)),
        "b_rel_cols": cols(L1_gnn_b_rel),
        "b_rel_row": np.asarray(L1_gnn_b_rel).reshape(1, REL * D),
        "w_ih_t": halves(np.ascontiguousarray(np.asarray(L1_gnn_W_ih).T)),
        "b_ih_cols": cols(L1_gnn_b_ih),
        "b_hh_cols": cols(L1_gnn_b_hh),
        "w_mlp1": halves(np.ascontiguousarray(np.asarray(L1_gnn_W1).T)),
        "b_mlp1": cols(L1_gnn_b1),
        "w_mlp2": np.ascontiguousarray(np.asarray(L1_gnn_W2).T),
        "b_mlp2": cols(L1_gnn_b2),
        "w_mlp3": np.ascontiguousarray(np.asarray(L1_gnn_W3).T),
        "b_mlp3": np.asarray(L1_gnn_b3).reshape(1, D),
    }
    nc = bacc.Bacc("TRN2", target_bir_lowering=False, num_devices=1)
    args = [nc.dram_tensor(name, a.shape, mybir.dt.from_np(a.dtype), kind="ExternalInput").ap()
            for name, a in arrays.items()]
    out = nc.dram_tensor("out", (N_NODES, D), F32, kind="ExternalOutput").ap()
    build(nc, *args, out)
    return run_bass_kernel_spmd(nc, [arrays], core_ids=[0]).results[0]["out"]
```
